# Optimizing a Trainium2 kernel written in Bass

```python
import numpy as np
import jax
import jax.numpy as jnp

def _softmax(x, axis=-1):
    return jax.nn.softmax(x, axis=axis)

def _gelu(x):
    return jax.nn.gelu(x, approximate=True)

def _silu(x):
    return jax.nn.silu(x)

def _sigmoid(x):
    return jax.nn.sigmoid(x)

def _layernorm(x, axis=-1, eps=1e-05):
    m = jnp.mean(x, axis=axis, keepdims=True)
    v = jnp.var(x, axis=axis, keepdims=True)
    return (x - m) / jnp.sqrt(v + eps)

def _scatter_add(tgt, idx, src, axis=0):
    return tgt.at[idx].add(src)

def _segment_sum(src, seg, n):
    return jax.ops.segment_sum(src, seg, n)
kernel_name = 'mk_decoder_postln_d2_seqx_r4_0ffa7b'

def setup_inputs(seed: int=0):
    np.random.seed(seed)
    _w = jnp.asarray

    def _rec_inputs():
        import jax
        import jax.numpy as jnp
        _rk = jax.random.key(seed)
        x = 4.136e-05 + 0.9999 * jax.random.normal(jax.random.fold_in(_rk, 1), (4, 512, 512), jnp.float32)
        _lenS = 512 - jax.random.randint(jax.random.fold_in(_rk, 7), (4,), 0, max(1, 512 // 4) + 1, jnp.int32)
        _lenS2 = 512 - jax.random.randint(jax.random.fold_in(_rk, 8), (4,), 0, max(1, 512 // 4) + 1, jnp.int32)
        _ctx_1024P = jax.random.normal(jax.random.fold_in(_rk, 11), (4, 16, 256), jnp.float32)
        _ctx_1024c = jax.random.dirichlet(jax.random.fold_in(_rk, 511), 0.3 * jnp.ones((16,), jnp.float32), (4, 512))
        _ctx_1024t = jnp.einsum('bsk,bkd->bsd', _ctx_1024c, _ctx_1024P)
        _ctx_1024t = _ctx_1024t * jax.lax.rsqrt(jnp.mean(jnp.square(_ctx_1024t)) + 1e-12) * 0.953939
        ctx_1024 = -0.000292821 + 1.00034 * (_ctx_1024t + 0.3 * jax.random.normal(jax.random.fold_in(_rk, 611), (4, 512, 256), jnp.float32))
        return (x, ctx_1024)
    x, ctx_1024 = _rec_inputs()

    def _L0_attn_setup():
        import jax, jax.numpy as jnp
        import numpy as np
        H, DI, N, K, R, FF = (512, 1024, 16, 4, 128, 1408)
        B, S = (2, 256)
        EPS = 1e-06

        def rmsnorm(x, w):
            v = jnp.mean(x * x, axis=-1, keepdims=True)
            return x * jax.lax.rsqrt(v + EPS) * w

        def causal_conv1d(x, w, b):
            y = jax.lax.conv_general_dilated(x.transpose(0, 2, 1), w, window_strides=(1,), padding=[(K - 1, 0)], dimension_numbers=('NCH', 'OIH', 'NCH'), feature_group_count=DI)
            return (y + b[None, :, None]).transpose(0, 2, 1)

        def selective_scan(u, A, Bm, Cm, Dp, dt):

            def step(h, xs):
                dt_t, B_t, C_t, u_t = xs
                dA = jnp.exp(dt_t[:, :, None] * A)
                dBu = dt_t[:, :, None] * B_t[:, None, :] * u_t[:, :, None]
                h = dA * h + dBu
                y = jnp.einsum('bdn,bn->bd', h, C_t)
                return (h, y)
            xs = (dt.transpose(1, 0, 2), Bm.transpose(1, 0, 2), Cm.transpose(1, 0, 2), u.transpose(1, 0, 2))
            h0 = jnp.zeros((u.shape[0], DI, N), u.dtype)
            _, ys = jax.lax.scan(step, h0, xs)
            return ys.transpose(1, 0, 2) + u * Dp
        key = jax.random.key(seed)
        ks = jax.random.split(key, 16)
        sc = 0.02
        inp = {'hidden_states': jax.random.normal(ks[0], (B, S, H), jnp.float32), 'input_ln_w': jnp.ones((H,), jnp.float32), 'w_in': jax.random.normal(ks[1], (2 * DI, H), jnp.float32) * sc, 'conv_w': jax.random.normal(ks[2], (DI, 1, K), jnp.float32) * 0.3, 'conv_b': jax.random.normal(ks[3], (DI,), jnp.float32) * sc, 'w_x': jax.random.normal(ks[4], (R + 2 * N, DI), jnp.float32) * sc, 'dt_ln_w': jnp.ones((R,), jnp.float32), 'b_ln_w': jnp.ones((N,), jnp.float32), 'c_ln_w': jnp.ones((N,), jnp.float32), 'w_dt': jax.random.normal(ks[5], (DI, R), jnp.float32) * sc, 'b_dt': jax.random.normal(ks[6], (DI,), jnp.float32) * sc - 4.0, 'A_log': jnp.broadcast_to(jnp.log(jnp.arange(1, N + 1, dtype=jnp.float32)), (DI, N)), 'D_skip': jnp.ones((DI,), jnp.float32), 'w_out': jax.random.normal(ks[7], (H, DI), jnp.float32) * sc, 'pre_ff_ln_w': jnp.ones((H,), jnp.float32), 'w_gate': jax.random.normal(ks[8], (FF, H), jnp.float32) * sc, 'w_up': jax.random.normal(ks[9], (FF, H), jnp.float32) * sc, 'w_down': jax.random.normal(ks[10], (H, FF), jnp.float32) * sc}
        return inp
    _L0_attn_all = _L0_attn_setup()
    _L0_attn_in = {k: v for k, v in _L0_attn_all.items() if k in ('input_ln_w', 'w_in', 'conv_w', 'conv_b', 'w_x', 'dt_ln_w', 'b_ln_w', 'c_ln_w', 'w_dt', 'b_dt', 'A_log', 'D_skip', 'w_out', 'pre_ff_ln_w', 'w_gate', 'w_up', 'w_down')}
    del _L0_attn_all

    def _L0_xattn_setup():
        import jax, jax.numpy as jnp
        import numpy as np
        import math
        B, L, DM = (2, 512, 256)
        DS, DC, EXP = (16, 4, 2)
        DI = EXP * DM
        DR = math.ceil(DM / 16)
        DT_MIN, DT_MAX, DT_FLOOR = (0.001, 0.1, 0.0001)

        def _ssm_forward(hidden_states, z, in_proj_w, conv_w, conv_b, x_proj_w, dt_proj_w, dt_proj_b, A_log, D):
            b = hidden_states.shape[0]
            x = jnp.einsum('ed,bld->bel', in_proj_w, hidden_states)
            xp = jnp.pad(x, ((0, 0), (0, 0), (DC - 1, 0)))
            xc = jax.lax.conv_general_dilated(xp, conv_w[:, None, :], window_strides=(1,), padding='VALID', dimension_numbers=('NCH', 'OIH', 'NCH'), feature_group_count=DI)
            u = jax.nn.silu(xc + conv_b[None, :, None])
            x_dbl = jnp.einsum('ke,bel->bkl', x_proj_w, u)
            dt_lo = x_dbl[:, :DR]
            Bm = x_dbl[:, DR:DR + DS]
            Cm = x_dbl[:, DR + DS:]
            delta = jax.nn.softplus(jnp.einsum('er,brl->bel', dt_proj_w, dt_lo) + dt_proj_b[None, :, None])
            A = -jnp.exp(A_log)

            def step(state, xs):
                d_t, B_t, C_t, u_t = xs
                dA = jnp.exp(d_t[..., None] * A)
                state = state * dA + (d_t * u_t)[..., None] * B_t[:, None, :]
                y_t = jnp.einsum('ben,bn->be', state, C_t)
                return (state, y_t)
            xs = (jnp.moveaxis(delta, -1, 0), jnp.moveaxis(Bm, -1, 0), jnp.moveaxis(Cm, -1, 0), jnp.moveaxis(u, -1, 0))
            state0 = jnp.zeros((b, DI, DS), delta.dtype)
            _, ys = jax.lax.scan(step, state0, xs)
            y = jnp.moveaxis(ys, 0, -1)
            y = y + D[None, :, None] * u
            y = y * jax.nn.silu(z)
            return jnp.swapaxes(y, 1, 2)
        key = jax.random.key(seed)
        ks = jax.random.split(key, 8)
        hidden_states = jax.random.normal(ks[0], (B, L, DM), jnp.float32)
        z = jax.random.normal(ks[1], (B, DI, L), jnp.float32)
        in_proj_w = jax.random.normal(ks[2], (DI, DM), jnp.float32) * DM ** (-0.5)
        conv_w = jax.random.normal(ks[3], (DI, DC), jnp.float32) * DC ** (-0.5)
        conv_b = jnp.zeros((DI,), jnp.float32)
        x_proj_w = jax.random.normal(ks[4], (DR + 2 * DS, DI), jnp.float32) * DI ** (-0.5)
        dt_std = DR ** (-0.5)
        dt_proj_w = jax.random.uniform(ks[5], (DI, DR), jnp.float32, -dt_std, dt_std)
        dt = jnp.exp(jax.random.uniform(ks[6], (DI,), jnp.float32) * (math.log(DT_MAX) - math.log(DT_MIN)) + math.log(DT_MIN))
        dt = jnp.clip(dt, DT_FLOOR)
        dt_proj_b = dt + jnp.log(-jnp.expm1(-dt))
        A_log = jnp.log(jnp.broadcast_to(jnp.arange(1, DS + 1, dtype=jnp.float32), (DI, DS)))
        D = jnp.ones((DI,), jnp.float32)
        return dict(hidden_states=hidden_states, z=z, in_proj_w=in_proj_w, conv_w=conv_w, conv_b=conv_b, x_proj_w=x_proj_w, dt_proj_w=dt_proj_w, dt_proj_b=dt_proj_b, A_log=A_log, D=D)
    _L0_xattn_all = _L0_xattn_setup()
    _L0_xattn_in = {k: v for k, v in _L0_xattn_all.items() if k in ('in_proj_w', 'conv_w', 'conv_b', 'x_proj_w', 'dt_proj_w', 'dt_proj_b', 'A_log', 'D')}
    del _L0_xattn_all

    def _L0_ffn_setup():
        import jax, jax.numpy as jnp
        import numpy as np
        B, S, H = (2, 256, 512)
        E, K, F = (8, 2, 352)
        N_SHARED = 2
        FS = F * N_SHARED
        ROUTED_SCALE = 1.0

        def _swiglu_mlp(x, wg, wu, wd):
            return jax.nn.silu(x @ wg.T) * (x @ wu.T) @ wd.T
        key = jax.random.key(seed)
        ks = jax.random.split(key, 8)

        def w(k, shape, fan_in):
            return jax.random.normal(k, shape, jnp.float32) * (1.0 / np.sqrt(fan_in))
        return {'hidden_states': jax.random.normal(ks[0], (B, S, H), jnp.float32), 'gate_weight': w(ks[1], (E, H), H), 'w_gate': w(ks[2], (E, F, H), H), 'w_up': w(ks[3], (E, F, H), H), 'w_down': w(ks[4], (E, H, F), F), 'sw_gate': w(ks[5], (FS, H), H), 'sw_up': w(ks[6], (FS, H), H), 'sw_down': w(ks[7], (H, FS), FS)}
    _L0_ffn_all = _L0_ffn_setup()
    _L0_ffn_in = {k: v for k, v in _L0_ffn_all.items() if k in ('gate_weight', 'w_gate', 'w_up', 'w_down', 'sw_gate', 'sw_up', 'sw_down')}
    del _L0_ffn_all

    def _L1_attn_setup():
        import jax, jax.numpy as jnp
        import numpy as np
        DIM = 512
        SEGMENT_LEN = 128
        HEADS = 32
        DIM_HEAD = 64
        P = 16
        SCALE = 1.0 / np.sqrt(DIM_HEAD)
        key = jax.random.key(seed)
        ks = jax.random.split(key, 4)
        seq = jax.random.normal(ks[0], (2, 2048, DIM), dtype=jnp.float32)
        w_norm = jnp.ones((DIM,), dtype=jnp.float32)
        w_qkv = jax.random.normal(ks[1], (DIM, 3 * HEADS * DIM_HEAD), dtype=jnp.float32) * 0.02
        w_out = jax.random.normal(ks[2], (HEADS * DIM_HEAD, DIM), dtype=jnp.float32) * 0.02
        pm = jax.random.normal(ks[3], (2, HEADS, P, DIM_HEAD), dtype=jnp.float32) * 0.02
        return {'seq': seq, 'w_norm': w_norm, 'w_qkv': w_qkv, 'w_out': w_out, 'pm': pm}
    _L1_attn_all = _L1_attn_setup()
    _L1_attn_in = {k: v for k, v in _L1_attn_all.items() if k in ('w_norm', 'w_qkv', 'w_out', 'pm')}
    del _L1_attn_all

    def _L1_xattn_setup():
        import jax, jax.numpy as jnp
        import numpy as np
        key = jax.random.key(seed)
        ks = jax.random.split(key, 6)
        B, L, N, C, D = (8, 128, 512, 256, 128)
        return {'teacher_logits': jax.random.normal(ks[0], (B, L, N), dtype=jnp.float32), 'teacher_features': jax.random.normal(ks[1], (B, N, C), dtype=jnp.float32), 'Wq': jax.random.normal(ks[2], (D, C), dtype=jnp.float32) * (1.0 / np.sqrt(C)), 'bq': jnp.zeros((D,), dtype=jnp.float32), 'Wk': jax.random.normal(ks[3], (D, C), dtype=jnp.float32) * (1.0 / np.sqrt(C)), 'bk': jnp.zeros((D,), dtype=jnp.float32)}
    _L1_xattn_all = _L1_xattn_setup()
    _L1_xattn_in = {k: v for k, v in _L1_xattn_all.items() if k in ('Wq', 'bq', 'Wk', 'bk')}
    del _L1_xattn_all

    def _L1_ffn_setup():
        import jax, jax.numpy as jnp
        import numpy as np
        TOP_K = 8
        key = jax.random.key(seed)
        k1, k2, k3 = jax.random.split(key, 3)
        B, S, H, E = (4, 1024, 512, 64)
        hidden_states = jax.random.normal(k1, (B, S, H), dtype=jnp.float32)
        router_weight = jax.random.normal(k2, (E, H), dtype=jnp.float32)
        router_bias = jnp.zeros((E,), dtype=jnp.float32)
        expert_bias = jax.random.normal(k3, (E, H), dtype=jnp.float32) * 0.1
        return {'hidden_states': hidden_states, 'router_weight': router_weight, 'router_bias': router_bias, 'expert_bias': expert_bias}
    _L1_ffn_all = _L1_ffn_setup()
    _L1_ffn_in = {k: v for k, v in _L1_ffn_all.items() if k in ('router_weight', 'router_bias', 'expert_bias')}
    del _L1_ffn_all
    return {'x': x, 'ctx_1024': ctx_1024, 'L0_attn_input_ln_w': _L0_attn_in['input_ln_w'], 'L0_attn_w_in': _L0_attn_in['w_in'], 'L0_attn_conv_w': _L0_attn_in['conv_w'], 'L0_attn_conv_b': _L0_attn_in['conv_b'], 'L0_attn_w_x': _L0_attn_in['w_x'], 'L0_attn_dt_ln_w': _L0_attn_in['dt_ln_w'], 'L0_attn_b_ln_w': _L0_attn_in['b_ln_w'], 'L0_attn_c_ln_w': _L0_attn_in['c_ln_w'], 'L0_attn_w_dt': _L0_attn_in['w_dt'], 'L0_attn_b_dt': _L0_attn_in['b_dt'], 'L0_attn_A_log': _L0_attn_in['A_log'], 'L0_attn_D_skip': _L0_attn_in['D_skip'], 'L0_attn_w_out': _L0_attn_in['w_out'], 'L0_attn_pre_ff_ln_w': _L0_attn_in['pre_ff_ln_w'], 'L0_attn_w_gate': _L0_attn_in['w_gate'], 'L0_attn_w_up': _L0_attn_in['w_up'], 'L0_attn_w_down': _L0_attn_in['w_down'], 'L0_xattn_in_proj_w': _L0_xattn_in['in_proj_w'], 'L0_xattn_conv_w': _L0_xattn_in['conv_w'], 'L0_xattn_conv_b': _L0_xattn_in['conv_b'], 'L0_xattn_x_proj_w': _L0_xattn_in['x_proj_w'], 'L0_xattn_dt_proj_w': _L0_xattn_in['dt_proj_w'], 'L0_xattn_dt_proj_b': _L0_xattn_in['dt_proj_b'], 'L0_xattn_A_log': _L0_xattn_in['A_log'], 'L0_xattn_D': _L0_xattn_in['D'], 'L0_ffn_gate_weight': _L0_ffn_in['gate_weight'], 'L0_ffn_w_gate': _L0_ffn_in['w_gate'], 'L0_ffn_w_up': _L0_ffn_in['w_up'], 'L0_ffn_w_down': _L0_ffn_in['w_down'], 'L0_ffn_sw_gate': _L0_ffn_in['sw_gate'], 'L0_ffn_sw_up': _L0_ffn_in['sw_up'], 'L0_ffn_sw_down': _L0_ffn_in['sw_down'], 'L1_attn_w_norm': _L1_attn_in['w_norm'], 'L1_attn_w_qkv': _L1_attn_in['w_qkv'], 'L1_attn_w_out': _L1_attn_in['w_out'], 'L1_attn_pm': _L1_attn_in['pm'], 'L1_xattn_Wq': _L1_xattn_in['Wq'], 'L1_xattn_bq': _L1_xattn_in['bq'], 'L1_xattn_Wk': _L1_xattn_in['Wk'], 'L1_xattn_bk': _L1_xattn_in['bk'], 'L1_ffn_router_weight': _L1_ffn_in['router_weight'], 'L1_ffn_router_bias': _L1_ffn_in['router_bias'], 'L1_ffn_expert_bias': _L1_ffn_in['expert_bias']}

def reference(x, ctx_1024, L0_attn_input_ln_w, L0_attn_w_in, L0_attn_conv_w, L0_attn_conv_b, L0_attn_w_x, L0_attn_dt_ln_w, L0_attn_b_ln_w, L0_attn_c_ln_w, L0_attn_w_dt, L0_attn_b_dt, L0_attn_A_log, L0_attn_D_skip, L0_attn_w_out, L0_attn_pre_ff_ln_w, L0_attn_w_gate, L0_attn_w_up, L0_attn_w_down, L0_xattn_in_proj_w, L0_xattn_conv_w, L0_xattn_conv_b, L0_xattn_x_proj_w, L0_xattn_dt_proj_w, L0_xattn_dt_proj_b, L0_xattn_A_log, L0_xattn_D, L0_ffn_gate_weight, L0_ffn_w_gate, L0_ffn_w_up, L0_ffn_w_down, L0_ffn_sw_gate, L0_ffn_sw_up, L0_ffn_sw_down, L1_attn_w_norm, L1_attn_w_qkv, L1_attn_w_out, L1_attn_pm, L1_xattn_Wq, L1_xattn_bq, L1_xattn_Wk, L1_xattn_bk, L1_ffn_router_weight, L1_ffn_router_bias, L1_ffn_expert_bias):
    import jax
    import jax.numpy as jnp

    def _L0_attn_ref(hidden_states, input_ln_w, w_in, conv_w, conv_b, w_x, dt_ln_w, b_ln_w, c_ln_w, w_dt, b_dt, A_log, D_skip, w_out, pre_ff_ln_w, w_gate, w_up, w_down):
        import jax, jax.numpy as jnp
        import numpy as np
        H, DI, N, K, R, FF = (512, 1024, 16, 4, 128, 1408)
        B, S = (2, 256)
        EPS = 1e-06

        def rmsnorm(x, w):
            v = jnp.mean(x * x, axis=-1, keepdims=True)
            return x * jax.lax.rsqrt(v + EPS) * w

        def causal_conv1d(x, w, b):
            y = jax.lax.conv_general_dilated(x.transpose(0, 2, 1), w, window_strides=(1,), padding=[(K - 1, 0)], dimension_numbers=('NCH', 'OIH', 'NCH'), feature_group_count=DI)
            return (y + b[None, :, None]).transpose(0, 2, 1)

        def selective_scan(u, A, Bm, Cm, Dp, dt):

            def step(h, xs):
                dt_t, B_t, C_t, u_t = xs
                dA = jnp.exp(dt_t[:, :, None] * A)
                dBu = dt_t[:, :, None] * B_t[:, None, :] * u_t[:, :, None]
                h = dA * h + dBu
                y = jnp.einsum('bdn,bn->bd', h, C_t)
                return (h, y)
            xs = (dt.transpose(1, 0, 2), Bm.transpose(1, 0, 2), Cm.transpose(1, 0, 2), u.transpose(1, 0, 2))
            h0 = jnp.zeros((u.shape[0], DI, N), u.dtype)
            _, ys = jax.lax.scan(step, h0, xs)
            return ys.transpose(1, 0, 2) + u * Dp
        residual = hidden_states
        x = rmsnorm(hidden_states, input_ln_w)
        proj = x @ w_in.T
        u, gate = jnp.split(proj, 2, axis=-1)
        u = jax.nn.silu(causal_conv1d(u, conv_w, conv_b))
        ssm_p = u @ w_x.T
        t_r, Bm, Cm = jnp.split(ssm_p, [R, R + N], axis=-1)
        t_r = rmsnorm(t_r, dt_ln_w)
        Bm = rmsnorm(Bm, b_ln_w)
        Cm = rmsnorm(Cm, c_ln_w)
        dt = jax.nn.softplus(t_r @ w_dt.T + b_dt)
        A = -jnp.exp(A_log)
        y = selective_scan(u, A, Bm, Cm, D_skip, dt)
        y = y * jax.nn.silu(gate)
        mixer_out = y @ w_out.T
        hidden = residual + mixer_out
        residual = hidden
        h = rmsnorm(hidden, pre_ff_ln_w)
        ff = jax.nn.silu(h @ w_gate.T) * (h @ w_up.T) @ w_down.T
        return residual + ff

    def _L0_xattn_ref(hidden_states, z, in_proj_w, conv_w, conv_b, x_proj_w, dt_proj_w, dt_proj_b, A_log, D):
        import jax, jax.numpy as jnp
        import numpy as np
        import math
        B, L, DM = (2, 512, 256)
        DS, DC, EXP = (16, 4, 2)
        DI = EXP * DM
        DR = math.ceil(DM / 16)
        DT_MIN, DT_MAX, DT_FLOOR = (0.001, 0.1, 0.0001)

        def _ssm_forward(hidden_states, z, in_proj_w, conv_w, conv_b, x_proj_w, dt_proj_w, dt_proj_b, A_log, D):
            b = hidden_states.shape[0]
            x = jnp.einsum('ed,bld->bel', in_proj_w, hidden_states)
            xp = jnp.pad(x, ((0, 0), (0, 0), (DC - 1, 0)))
            xc = jax.lax.conv_general_dilated(xp, conv_w[:, None, :], window_strides=(1,), padding='VALID', dimension_numbers=('NCH', 'OIH', 'NCH'), feature_group_count=DI)
            u = jax.nn.silu(xc + conv_b[None, :, None])
            x_dbl = jnp.einsum('ke,bel->bkl', x_proj_w, u)
            dt_lo = x_dbl[:, :DR]
            Bm = x_dbl[:, DR:DR + DS]
            Cm = x_dbl[:, DR + DS:]
            delta = jax.nn.softplus(jnp.einsum('er,brl->bel', dt_proj_w, dt_lo) + dt_proj_b[None, :, None])
            A = -jnp.exp(A_log)

            def step(state, xs):
                d_t, B_t, C_t, u_t = xs
                dA = jnp.exp(d_t[..., None] * A)
                state = state * dA + (d_t * u_t)[..., None] * B_t[:, None, :]
                y_t = jnp.einsum('ben,bn->be', state, C_t)
                return (state, y_t)
            xs = (jnp.moveaxis(delta, -1, 0), jnp.moveaxis(Bm, -1, 0), jnp.moveaxis(Cm, -1, 0), jnp.moveaxis(u, -1, 0))
            state0 = jnp.zeros((b, DI, DS), delta.dtype)
            _, ys = jax.lax.scan(step, state0, xs)
            y = jnp.moveaxis(ys, 0, -1)
            y = y + D[None, :, None] * u
            y = y * jax.nn.silu(z)
            return jnp.swapaxes(y, 1, 2)
        return _ssm_forward(hidden_states, z, in_proj_w, conv_w, conv_b, x_proj_w, dt_proj_w, dt_proj_b, A_log, D)

    def _L0_ffn_ref(hidden_states, gate_weight, w_gate, w_up, w_down, sw_gate, sw_up, sw_down):
        import jax, jax.numpy as jnp
        import numpy as np
        B, S, H = (2, 256, 512)
        E, K, F = (8, 2, 352)
        N_SHARED = 2
        FS = F * N_SHARED
        ROUTED_SCALE = 1.0

        def _swiglu_mlp(x, wg, wu, wd):
            return jax.nn.silu(x @ wg.T) * (x @ wu.T) @ wd.T
        b, s, h = hidden_states.shape
        x = hidden_states.reshape(-1, h)
        T = x.shape[0]
        logits = x.astype(jnp.float32) @ gate_weight.astype(jnp.float32).T
        scores = jax.nn.softmax(logits, axis=-1)
        topk_w, topk_idx = jax.lax.top_k(scores, K)
        topk_w = topk_w / (jnp.sum(topk_w, axis=-1, keepdims=True) + 1e-20)
        topk_w = topk_w * ROUTED_SCALE
        cw = jnp.zeros((T, E), jnp.float32).at[jnp.arange(T)[:, None], topk_idx].add(topk_w)
        g = jax.nn.silu(jnp.einsum('th,efh->tef', x, w_gate)) * jnp.einsum('th,efh->tef', x, w_up)
        expert_out = jnp.einsum('tef,ehf->teh', g, w_down)
        y = jnp.einsum('te,teh->th', cw, expert_out).reshape(b, s, h)
        y = y + _swiglu_mlp(x, sw_gate, sw_up, sw_down).reshape(b, s, h)
        return y

    def _L1_attn_ref(seq, w_norm, w_qkv, w_out, pm):
        import jax, jax.numpy as jnp
        import numpy as np
        DIM = 512
        SEGMENT_LEN = 128
        HEADS = 32
        DIM_HEAD = 64
        P = 16
        SCALE = 1.0 / np.sqrt(DIM_HEAD)
        b, seq_len, d = seq.shape
        next_len = -(-seq_len // SEGMENT_LEN) * SEGMENT_LEN
        pad = next_len - seq_len
        x = jnp.pad(seq, ((0, 0), (0, pad), (0, 0))) if pad > 0 else seq
        w = next_len // SEGMENT_LEN
        x = x.reshape(b * SEGMENT_LEN, w, d)
        eps = jnp.finfo(x.dtype).eps
        x = x * jax.lax.rsqrt(jnp.mean(jnp.square(x), axis=-1, keepdims=True) + eps) * w_norm
        qkv = x @ w_qkv
        q, k, v = jnp.split(qkv, 3, axis=-1)
        B = x.shape[0]
        split = lambda t: t.reshape(B, w, HEADS, DIM_HEAD).transpose(0, 2, 1, 3)
        q, k, v = (split(q), split(k), split(v))
        pmk = jnp.broadcast_to(pm[0], (B, HEADS, P, DIM_HEAD))
        pmv = jnp.broadcast_to(pm[1], (B, HEADS, P, DIM_HEAD))
        k = jnp.concatenate([pmk, k], axis=2)
        v = jnp.concatenate([pmv, v], axis=2)
        scores = jnp.einsum('bhqd,bhkd->bhqk', q, k) * SCALE
        mask = jnp.arange(P + w)[None, :] <= jnp.arange(w)[:, None]
        scores = jnp.where(mask, scores, jnp.finfo(scores.dtype).min)
        attn = jax.nn.softmax(scores, axis=-1)
        out = jnp.einsum('bhqk,bhkd->bhqd', attn, v)
        out = out.transpose(0, 2, 1, 3).reshape(B, w, HEADS * DIM_HEAD)
        out = out @ w_out
        out = out.reshape(b, SEGMENT_LEN * w, d)
        return out[:, :seq_len]

    def _L1_xattn_ref(teacher_logits, teacher_features, Wq, bq, Wk, bk):
        import jax, jax.numpy as jnp
        import numpy as np
        query = jnp.einsum('bnc,dc->bnd', teacher_features, Wq) + bq
        key = jnp.einsum('bnc,dc->bnd', teacher_features, Wk) + bk
        energy = jnp.einsum('bnd,bmd->bnm', query, key)
        attention = jax.nn.softmax(energy, axis=-1)
        x_m = jnp.einsum('bln,bmn->blm', teacher_logits, attention)
        return x_m

    def _L1_ffn_ref(hidden_states, router_weight, router_bias, expert_bias):
        import jax, jax.numpy as jnp
        import numpy as np
        TOP_K = 8
        B, S, H = hidden_states.shape
        flat = hidden_states.reshape(B * S, H)
        logits = jnp.einsum('th,eh->te', flat, router_weight) + router_bias
        scores = jax.nn.softmax(logits, axis=-1)
        topk_w, topk_idx = jax.lax.top_k(scores, TOP_K)
        gathered_bias = expert_bias[topk_idx]
        out = flat * jnp.sum(topk_w, axis=-1, keepdims=True) + jnp.einsum('tk,tkh->th', topk_w, gathered_bias)
        return out.reshape(B, S, H)
    x = _layernorm(x + _L0_attn_ref(x, L0_attn_input_ln_w, L0_attn_w_in, L0_attn_conv_w, L0_attn_conv_b, L0_attn_w_x, L0_attn_dt_ln_w, L0_attn_b_ln_w, L0_attn_c_ln_w, L0_attn_w_dt, L0_attn_b_dt, L0_attn_A_log, L0_attn_D_skip, L0_attn_w_out, L0_attn_pre_ff_ln_w, L0_attn_w_gate, L0_attn_w_up, L0_attn_w_down), axis=-1)
    x = _layernorm(x + _L0_xattn_ref(ctx_1024, x, L0_xattn_in_proj_w, L0_xattn_conv_w, L0_xattn_conv_b, L0_xattn_x_proj_w, L0_xattn_dt_proj_w, L0_xattn_dt_proj_b, L0_xattn_A_log, L0_xattn_D), axis=-1)
    x = _layernorm(x + _L0_ffn_ref(x, L0_ffn_gate_weight, L0_ffn_w_gate, L0_ffn_w_up, L0_ffn_w_down, L0_ffn_sw_gate, L0_ffn_sw_up, L0_ffn_sw_down), axis=-1)
    x = _layernorm(x + _L1_attn_ref(x, L1_attn_w_norm, L1_attn_w_qkv, L1_attn_w_out, L1_attn_pm), axis=-1)
    x = _layernorm(x + _L1_xattn_ref(x, ctx_1024, L1_xattn_Wq, L1_xattn_bq, L1_xattn_Wk, L1_xattn_bk), axis=-1)
    x = _layernorm(x + _L1_ffn_ref(x, L1_ffn_router_weight, L1_ffn_router_bias, L1_ffn_expert_bias), axis=-1)
    return x

_drawn_inputs = setup_inputs


def setup_inputs(seed=0):
    import zlib

    import numpy as np

    out = dict(_drawn_inputs(seed))
    spreads = {'L0_attn_input_ln_w': (1.0, 0.6),
     'L0_attn_dt_ln_w': (1.0, 0.6),
     'L0_attn_b_ln_w': (1.0, 0.6),
     'L0_attn_c_ln_w': (1.0, 0.6),
     'L0_attn_D_skip': (1.0, 0.6),
     'L0_attn_pre_ff_ln_w': (1.0, 0.2),
     'L0_xattn_conv_b': (0.0, 0.1),
     'L0_xattn_D': (1.0, 0.2),
     'L1_attn_w_norm': (1.0, 0.6),
     'L1_xattn_bq': (0.0, 0.1),
     'L1_xattn_bk': (0.0, 0.8),
     'L1_ffn_router_bias': (0.0, 0.8)}
    factors = {'L0_attn_conv_b': 7.994,
     'L0_attn_w_x': 4.147,
     'L0_attn_w_dt': 8.0,
     'L0_attn_b_dt': 8.0,
     'L0_attn_A_log': 5.522,
     'L1_attn_w_qkv': 8.0,
     'L1_attn_w_out': 4.136,
     'L1_attn_pm': 4.215}
    for name, (base, spread) in spreads.items():
        noise = np.random.default_rng([zlib.crc32(name.encode()), seed]).standard_normal(out[name].shape)
        drawn = base * np.exp(spread * noise) if base else spread * noise
        out[name] = jnp.asarray(drawn.astype(out[name].dtype))
    for name, factor in factors.items():
        out[name] = (out[name] * factor).astype(out[name].dtype)
    return out
```

```python
import concourse.bass as bass
from concourse import mybir
from contextlib import ExitStack

P = 128
SEQS, TOK, HID = 4, 512, 512
KC = HID // P
TT = TOK // P
DI, NST, RANK, TAPS = 1024, 16, 128, 4
UC = DI // P
CTX, DIB, RANKB = 256, 512, 16
CC = CTX // P
FF = 1408
FA = FF // P
EXP, FE, FS = 8, 352, 704
ROUTED = EXP * FE // P
FC = -(-(EXP * FE + FS) // P)
MIXED = [c for c in range(ROUTED) if c * P // FE != (c * P + P - 1) // FE]
PASSES = [(0, 10), (10, 20), (20, FC)]
HIDMAX = FA
HEADS, DH, SEG = 32, 64, 4
EXR, TOPR = 64, 8
NSLOT, SLOT = 7, 1024
BC = 2 * NST
EPS, EPS_LN = 1e-6, 1e-5
EPS_SEG = 1.1920929e-07
NEG = -3.0e38

_PACK = [("in_ln", KC), ("pre_ln", KC), ("conv_bA", UC), ("conv_wA", UC * TAPS), ("dt_bA", UC),
         ("DA", UC), ("A_logA", UC * NST), ("dt_ln", 1), ("bc_ln", 1), ("conv_bB", 4),
         ("conv_wB", 4 * TAPS), ("dt_bB", 4), ("DB", 4), ("A_logB", 4 * NST), ("seg_ln", KC),
         ("bq", 1), ("bk", 1), ("eps", 3), ("mask", SEG), ("iota", EXP), ("blk", BC),
         ("group", FC * 4), ("ident", P), ("gate", KC * EXP), ("router", KC * EXR), ("rbias", EXR),
         ("ones", P)]
COL = {}
PACK = 0
for _n, _c in _PACK:
    COL[_n] = PACK
    PACK += _c


def unit(q):
    return [("h_dt", q)] + [("h_scan", NST * q + n) for n in range(NST)] + [("h_fin", q)]


def hidden(kind, chunks):
    out = []
    for c in chunks:
        out.append((kind + "_mm", c))
        if c > chunks[0]:
            out.append((kind + "_ev", c - 1))
    return out + [(kind + "_ev", chunks[-1])]


COST = {"ffn_mm": 7, "exp_mm": 7, "ffn_down": 37, "exp_down": 34, "ln_a": 4, "ln_b": 6, "gate": 8,
        "route": 10, "att_qk": 5, "att_row": 2, "seg": 14, "xmix": 14, "bias": 20}


def merge(a, b):
    total = sum(COST.get(t, 0) for t, _ in b)
    done, out, b = 0.0, [], list(b)
    for i, step in enumerate(a):
        out.append(step)
        while b and (done < total * (i + 1) / len(a) or b[0][0] not in COST):
            done += COST.get(b[0][0], 0)
            out.append(b.pop(0))
    return out + b


def schedule(head, tail):
    order = []
    proj = [("h_norm", 0)] + [("h_proj", j) for j in range(2 * UC)] + [("h_bc", 0)] if head else []
    scans = unit(tail) + unit(tail + 1) if head else []
    if not tail:
        return proj + scans
    order += [("h_ctx", j) for j in range(4)] + [("mix", 0), ("h_ctxbc", 0), ("t_norm", 0)]
    order += merge(unit(0), hidden("ffn", range(FA)) + [("ffn_down", 0), ("ln_a", 0), ("ln_b", 0)])
    middle = [("gate", 0), ("ln_a", 1), ("ln_b", 1), ("route", 0)]
    order += merge(proj, middle)
    rest = []
    for p, (lo, hi) in enumerate(PASSES):
        rest += hidden("exp", range(lo, hi)) + [("exp_down", p)]
    rest += [("ln_a", 2), ("att_qk", 0), ("ln_b", 2)] + [("att_row", t) for t in range(TT)]
    rest += [("seg", 0), ("ln_a", 3), ("ln_b", 3), ("xmix", 0), ("ln_a", 4), ("ln_b", 4), ("bias", 0)]
    return order + merge(scans, rest)


SIGNALS = (
    [f"slot{i}" for i in range(NSLOT)] + ["x_in", "hx_in", "ctx_in", "tctx_in", "out_done"] +
    ["h_stat", "h_mm", "h_tr", "h_tstat", "h_bstat", "h_dtm", "b_row", "c_row",
     "h_sq", "h_ln", "h_rstd", "h_up", "h_th", "h_bsq", "dt_abs", "dt_exp", "dt_log", "da",
     "h_xn", "h_tap", "h_conv", "h_u", "h_gz", "h_tn", "h_bcf", "h_bc", "dt_one", "dt_res", "delta",
     "dbu", "scan", "hc", "h_y", "h_done", "pads", "firsts", "acc", "du"] +
    ["mm", "gu", "fold", "down", "mean", "stat", "nat", "route", "cwt", "cwb", "qk", "en", "en_t", "score",
     "att_t", "wt_t",
     "sq", "ln", "rstd", "th", "rexp", "qk_sb", "en_exp", "seg_exp", "att_sb", "fexp", "xs",
     "x1", "xn", "sg", "su", "hid", "v", "vpart", "cen", "x", "gz", "g1", "g2", "rt", "cw", "cwr", "en_max",
     "en_rec", "sg_s", "sg_p", "ft", "wm", "wt", "bn", "y", "resid", "att"])


def build(nc, pack, w_in, w_x, w_bc, w_dt, x_in_w, x_proj_w, x_dt_w, w_out, w_fgu, w_fdn, w_egu, w_edn,
          w_qk, ebias, wq_t, wo, pm, xT, ctxT, out):
    f32, f32r, u32 = mybir.dt.float32, mybir.dt.float32r, mybir.dt.uint32
    ALU, ACT, AX = mybir.AluOpType, mybir.ActivationFunctionType, mybir.AxisListType
    with ExitStack() as ctx:
        def sb(name, shape, dt=f32):
            return ctx.enter_context(nc.sbuf_tensor(name, shape, dt))

        s = {n: ctx.enter_context(nc.semaphore(n)) for n in SIGNALS}
        every = range(min(x.num for x in s.values()), max(x.num for x in s.values()) + 1)
        ps = ctx.enter_context(nc.psum_tensor("ps", [P, 8, 512], f32))

        pk = sb("pk", [P, PACK])
        wseg = sb("wseg", [P, KC, P])
        pseg = sb("pseg", [P, HID])
        eb = sb("eb", [EXR, HID])
        sel = sb("sel", [2 * BC, BC], f32r)
        selE = sb("selE", [64, FC * 4], f32r)
        selM = sb("selM", [64, len(MIXED), P], f32r)
        cwr = sb("cwr", [64, TOK], f32r)
        ring = sb("ring", [P, NSLOT, SLOT])
        ucv = sb("ucv", [P, UC, TOK])
        yg = sb("yg", [P, UC, TOK])
        yb = sb("yb", [P, 4, TOK])
        dl = sb("dl", [P, 4, TOK])
        du = sb("du", [P, 4, TOK])
        ya = sb("ya", [P, 4, TOK])
        da = sb("da", [P, 2, 4 * TOK])
        hb = sb("hb", [P, 2, 4 * TOK])
        hr = sb("hr", [P, TOK])
        tn = sb("tn", [P, TOK])
        bcf = sb("bcf", [BC, TOK])
        bcr = sb("bcr", [2 * BC, TOK], f32r)
        X = sb("X", [P, KC, TOK])
        V = sb("V", [P, KC, TOK])
        T1 = sb("T1", [P, KC, TOK])
        T2 = sb("T2", [P, KC, TOK])
        R = sb("R", [P, TOK])
        hid = sb("hid", [P, HIDMAX, TOK])
        sm = sb("sm", [P, 256])

        def c(name, i=0, n=1, parts=P):
            return pk[0:parts, COL[name] + i:COL[name] + i + n]

        def dav(i):
            return da[:, i, :].rearrange("p (c t) -> p c t", t=TOK)

        def hbv(i):
            return hb[:, i, :].rearrange("p (c t) -> p c t", t=TOK)

        ident, ones = c("ident", 0, P), c("ones", 0, P)
        hx = dav(0)
        up = hb[:, 1, 0:2 * (TOK + 3)].rearrange("p (i t) -> p i t", t=TOK + 3)
        cv = dav(1)[:, 0:2, :]
        ht = dav(1)[:, 2:4, :]
        cx = dav(0)[:, 0:CC, :]
        att = hid[:, 0:4, :]
        qT, kT = hid[:, 4, :], hid[:, 5, :]
        tcx = hid[:, 6:6 + CC, :]
        S = hid[:, 8, :]
        aT = hid[:, 9, :]
        th = T1[:, 0:2, :]

        def erow(n):
            return hid[:, 9 + n % 2, :]

        at = [0]

        def small(n):
            at[0] += n
            return sm[:, at[0] - n:at[0]]

        rm, re, rp, rf, ra, rb, rc = (small(TT * EXP).rearrange("p (t e) -> p t e", e=EXP) for _ in range(7))
        rs = small(TT)
        rw = small(TT * 2).rearrange("p (t e) -> p t e", e=2)
        r4, nmax, esum = small(TT), small(TT), small(TT)
        ri = sb("ri", [P, TT, EXP], u32)
        smx = sb("smx", [P, P])
        fl = hid[:, 6, 0:TT * EXR].rearrange("p (t e) -> p t e", e=EXR)
        fr = hid[:, 6, TT * EXR:2 * TT * EXR].rearrange("p (t e) -> p t e", e=EXR)
        fw = hid[:, 7, 0:TT * EXR].rearrange("p (t e) -> p t e", e=EXR)
        wT = hid[0:EXR, 10, :]
        bn = sb("bn", [P, TT, 6])
        mv = sb("mv", [P, TT, 2])
        Aneg = sb("Aneg", [P, 12, NST])

        def wide(ap, n):
            return ap.unsqueeze(1).to_broadcast([ap.shape[0], n, ap.shape[-1]])

        BDk = hid[:, 0, 0:128].rearrange("p (c j) -> p c j", j=8)
        BDv = hid[:, 2:6, :].rearrange("p a t -> p (a t)").rearrange("p (c m) -> p c m", m=P)
        BDn = hid[:, 1, 0:128].rearrange("p (c j) -> p c j", j=8)
        with nc.Block() as block:
            @block.sync
            def _(sp):
                sp.dma_start(pk[:, :], pack).then_inc(s["x_in"], 16)
                sp.dma_start(eb[:, :], ebias).then_inc(s["x_in"], 16)
                for r in range(4):
                    if r:
                        sp.wait_ge(s["mm"], r)
                    for q in range(4):
                        k = 4 * r + q
                        sp.dma_start(ring[:, q, 0:HID], wq_t[k]).then_inc(s["slot0"], 16)
                        sp.dma_start(ring[:, q, HID:], wo[k]).then_inc(s["slot0"], 16)

            @block.gpsimd
            def _(pool):
                pool.memset(BDk[:, :, :], 0.0).then_inc(s["pads"], 1)
                pool.memset(BDn[:, :, :], 0.0).then_inc(s["pads"], 1)
                pool.memset(BDv[:, :, :], 0.0).then_inc(s["pads"], 1)
                pool.memset(cwr[:, :].bitcast(u32), 0).then_inc(s["pads"], 1)

            @block.scalar
            def _(act):
                act.wait_ge(s["pads"], 4)
                for h2 in range(2):
                    for kv, dst in ((0, BDk), (1, BDn)):
                        act.dma_start(dst[64 * h2:64 * h2 + 64, :, SEG * h2:SEG * h2 + SEG],
                                      pm[kv, 64 * h2:64 * h2 + 64, :, 0:SEG]).then_inc(s["ctx_in"], 16)
                act.wait_ge(s["x_in"], 32)
                act.activation(Aneg[:, 0:UC, :].rearrange("p c n -> p (c n)"), c("A_logA", 0, UC * NST),
                               ACT.Exp).then_inc(s["sq"], 1)
                act.activation(Aneg[:, UC:, :].rearrange("p c n -> p (c n)"), c("A_logB", 0, 4 * NST),
                               ACT.Exp).then_inc(s["sq"], 1)

            @block.vector
            def _(dve):
                dve.wait_ge(s["x_in"], 32)
                dve.wait_ge(s["sq"], 2)
                dve.tensor_scalar(Aneg[:, :, :], Aneg[:, :, :], -1.0, None, ALU.mult)
                for name, n in (("conv_bA", UC), ("conv_wA", UC * TAPS), ("conv_bB", 4), ("conv_wB", 4 * TAPS)):
                    dve.tensor_scalar(c(name, 0, n), c(name, 0, n), 0.5, None, ALU.mult)
                dve.tensor_copy(sel[0:BC, :], c("ident", 0, BC, BC))
                dve.tensor_copy(sel[BC:2 * BC, :], c("ident", 0, BC, BC))
                dve.tensor_copy(selE[:, :], c("group", 0, FC * 4, 64))
                for i, k in enumerate(MIXED):
                    dve.tensor_copy(selM[:, i, :].rearrange("p (a b) -> p a b", b=32),
                                    c("group", 4 * k, 4, 64).unsqueeze(2).to_broadcast([64, 4, 32]))
                dve.wait_ge(s["ctx_in"], 64)
                dve.wait_ge(s["pads"], 4)
                for k in range(16):
                    last = dve.tensor_copy(BDv[:, k, 8 * k:8 * k + 8], BDn[:, k, :])
                last.then_inc(s["h_conv"], 1)
                dve.wait_ge(s["mm"], 4)
                for k in range(KC):
                    dve.tensor_scalar(wseg[:, k, :], ps[:, k, 0:P], c("seg_ln", k), float(DH) ** -0.5,
                                      ALU.mult, ALU.mult)
                dve.tensor_copy(pseg[:, :], ps[:, 4, :])

            @block.tensor
            def _(pe):
                pe.wait_ge(s["ctx_in"], 64)
                pe.wait_ge(s["h_conv"], 1)
                for r in range(4):
                    pe.wait_ge(s["slot0"], 128 * (r + 1))
                    for q in range(4):
                        k = 4 * r + q
                        for m in range(KC):
                            pe.matmul(ps[:, m, 8 * k:8 * k + 8], ring[:, q, m * P:(m + 1) * P],
                                      BDk[:, k, :], start=True, stop=True)
                        last = pe.matmul(ps[:, 4, :], BDv[:, k, :], ring[:, q, HID:],
                                         start=(k == 0), stop=(k == 15))
                    last.then_inc(s["mm"], 1)
        nc.all_engine_barrier(sems_to_clear=every)

        def loads(order, tail):
            fold, down, n = 0, 0, []
            for t, i in order:
                if t == "h_proj" and i % 2 == 0:
                    n.append((w_in[i // 2], "h_mm", 4 * tail + i + 2))
                elif t == "h_bc":
                    n.append((w_x, "h_tr", 2 * tail + 1))
                    n.append((w_bc, "h_tr", 2 * tail + 2))
                elif t == "h_dt":
                    a = i - tail
                    n.append((w_dt[:, 512 * a:512 * a + 512] if a >= 0 else x_dt_w, "h_dtm", 4 * i + 4))
                elif t == "h_ctx" and i == 0:
                    n.append((x_in_w, "h_mm", 4))
                elif t == "h_ctxbc":
                    n.append((x_proj_w, "h_tr", 2))
                elif t == "mix":
                    n += [(w_out[m], "mm", m + 1) for m in range(KC)]
                elif t == "ffn_mm":
                    n.append((w_fgu[i], "gu", i + 1))
                elif t == "exp_mm":
                    n.append((w_egu[i], "gu", FA + i + 1))
                elif t in ("ffn_down", "exp_down"):
                    lo, hi = (0, FA) if t == "ffn_down" else PASSES[i]
                    w = w_fdn if t == "ffn_down" else w_edn
                    down += KC
                    for k in range(lo, hi, 2):
                        m = min(2, hi - k)
                        src = w[k:k + m].rearrange("c p m -> p c m")
                        if k + m < hi:
                            fold += 1
                            n.append((src, "fold", fold))
                        else:
                            n.append((src, "down", down))
                elif t == "att_qk":
                    n.append((w_qk, "qk", 2))
            return n

        def run(bh, bt):
            head, tail = bh is not None, int(bt is not None)
            order = schedule(head, tail)

            with nc.Block(no_gpsimd_drain=True) as block:
                @block.sync
                def _(sp):
                    if tail:
                        sp.dma_start(cx, ctxT[bass.ds(bt, 1)].rearrange("b p k t -> (b p) k t")).then_inc(s["ctx_in"], 16)
                        sp.dma_start(X[:, :, :], xT[bass.ds(bt, 1)].rearrange("b p k t -> (b p) k t")).then_inc(s["x_in"], 16)
                    todo = loads(order, tail)
                    for k, (src, name, value) in enumerate(todo):
                        if k >= NSLOT:
                            sp.wait_ge(s[todo[k - NSLOT][1]], todo[k - NSLOT][2])
                        shape = src.shape
                        if len(shape) == 3:
                            dst = ring[:, k % NSLOT, 0:shape[1] * shape[2]].rearrange("p (a m) -> p a m", m=shape[2])
                        else:
                            dst = ring[0:shape[0], k % NSLOT, 0:shape[1]]
                        sp.dma_start(dst, src).then_inc(s[f"slot{k % NSLOT}"], 16)
                    if tail:
                        for t in range(TT):
                            sp.wait_ge(s["y"], t + 1)
                            sp.dma_start(out[bass.ds(bt, 1), t * P:(t + 1) * P, :].rearrange("b p h -> (b p) h"),
                                         V[:, t, :]).then_inc(s["out_done"], 16)
                        sp.wait_ge(s["out_done"], 16 * TT)

                @block.tensor
                def _(pe):
                    used = [0]
                    lnk = [0]
                    folds = [0]

                    def slot():
                        k = used[0]
                        used[0] += 1
                        pe.wait_ge(s[f"slot{k % NSLOT}"], 16 * (k // NSLOT + 1))
                        return ring[:, k % NSLOT, :]

                    cur = {}

                    def turn(n):
                        pe.wait_ge(s["en_exp"], n + 1)
                        if n:
                            pe.wait_ge(s["att"], n)
                        for k in range(KC):
                            i = pe.transpose(ps[:, 2, k * P:(k + 1) * P], erow(n)[:, k * P:(k + 1) * P], ident)
                        i.then_inc(s["en_t"], 1)

                    def down(lo, hi, done):
                        for k in range(lo, hi):
                            if (k - lo) % 2 == 0:
                                w = slot()
                            base = (k - lo) % 2 * HID
                            for m in range(KC):
                                if m == 0:
                                    pe.wait_ge(s["hid"], done + hi - lo if k == lo else done + k - lo + 1)
                                i = pe.matmul(ps[:, m, :], w[:, base + m * P:base + (m + 1) * P], hid[:, k - lo, :],
                                              start=(k == lo), stop=(k == hi - 1))
                                if k == hi - 1:
                                    i.then_inc(s["down"], 1)
                            if (k - lo) % 2 == 1 and k < hi - 1:
                                i.then_inc(s["fold"], 1)

                    for t, n in order:
                        if t == "h_norm":
                            if tail:
                                pe.wait_ge(s["hc"], NST)
                            for k in range(KC):
                                pe.wait_ge(s["h_sq"], k + 1)
                                i = pe.matmul(ps[:, 5, :], ones, hbv(0)[:, k, :], start=(k == 0), stop=(k == KC - 1))
                            i.then_inc(s["h_stat"], 1)
                        elif t == "h_proj":
                            if n % 2 == 0:
                                cur["h"] = slot()
                            if n == 0:
                                pe.wait_ge(s["h_ln"], 1)
                            elif n >= 3:
                                if n - 3 < UC:
                                    pe.wait_ge(s["h_up"], 4 * tail + n - 2)
                                else:
                                    pe.wait_ge(s["h_gz"], n - 2 - UC)
                            for k in range(KC):
                                if n == 0:
                                    pe.wait_ge(s["h_xn"], k + 1)
                                o = (n % 2) * KC * P + k * P
                                i = pe.matmul(ps[:, 5 + n % 3, :], cur["h"][:, o:o + P], hx[:, k, :],
                                              start=(k == 0), stop=(k == KC - 1))
                            i.then_inc(s["h_mm"], 1)
                        elif t == "h_bc":
                            w = slot()
                            pe.wait_ge(s["h_gz"], UC)
                            for k in range(UC):
                                pe.wait_ge(s["h_u"], 4 * tail + k + 1)
                                i = pe.matmul(ps[:, 5, :], w[:, k * P:(k + 1) * P], ucv[:, k, :],
                                              start=(k == 0), stop=(k == UC - 1))
                            i.then_inc(s["h_tr"], 1)
                            w = slot()
                            for k in range(UC):
                                i = pe.matmul(ps[0:BC, 6, :], w[:, k * BC:(k + 1) * BC], ucv[:, k, :],
                                              start=(k == 0), stop=(k == UC - 1))
                            i.then_inc(s["h_tr"], 1)
                            pe.wait_ge(s["h_bsq"], 1)
                            pe.matmul(ps[:, 7, :], ones, tn[:, :], start=True, stop=True).then_inc(s["h_tstat"], 1)
                            pe.wait_ge(s["h_tn"], tail + 1)
                            pe.wait_ge(s["h_bsq"], 2)
                            pe.matmul(ps[0:BC, 5, :], c("blk", 0, BC, BC), bcf[:, :], start=True, stop=True)\
                                .then_inc(s["h_bstat"], 1)
                        elif t == "h_ctx":
                            if n == 0:
                                cur["h"] = slot()
                                pe.wait_ge(s["ctx_in"], 16)
                            if n == 3:
                                pe.wait_ge(s["h_up"], 1)
                            for k in range(CC):
                                o = (n * CC + k) * P
                                i = pe.matmul(ps[:, 5 + n % 3, :], cur["h"][:, o:o + P], cx[:, k, :],
                                              start=(k == 0), stop=(k == CC - 1))
                            i.then_inc(s["h_mm"], 1)
                        elif t == "h_ctxbc":
                            w = slot()
                            pe.wait_ge(s["h_up"], 4)
                            for part, lo, m in ((5, 0, RANKB), (6, RANKB, BC)):
                                for k in range(4):
                                    if part == 5:
                                        pe.wait_ge(s["h_u"], k + 1)
                                    i = pe.matmul(ps[0:m, part, :], w[:, k * 48 + lo:k * 48 + lo + m], ucv[:, k, :],
                                                  start=(k == 0), stop=(k == 3))
                                i.then_inc(s["h_tr"], 1)
                        elif t == "h_dt":
                            w = slot()
                            a = n - tail
                            rows = P if a >= 0 else RANKB
                            if a == 0:
                                pe.wait_ge(s["h_ln"], 3)
                                pe.wait_ge(s["h_bcf"], 1)
                            elif a == 1:
                                pe.wait_ge(s["hc"], NST * n)
                            else:
                                pe.wait_ge(s["h_tn"], 1)
                                pe.wait_ge(s["h_bc"], 2)
                            for k in range(4):
                                if k == 3:
                                    pe.wait_ge(s["dt_abs"], 4 * n + 1)
                                pe.matmul(ps[:, 5 + k % 3, :], w[0:rows, k * P:(k + 1) * P], tn[0:rows, :],
                                          start=True, stop=True).then_inc(s["h_dtm"], 1)
                        elif t == "h_scan":
                            u, m = divmod(n, NST)
                            if m == 0:
                                pe.wait_ge(s["dt_abs"], 4 * u + 4)
                                pe.wait_ge(s["h_bc"], 2 if u - tail < 0 else 2 * tail + 2)
                                pe.matmul(ps[:, 5 + n % 2, :], sel[:, 0:1].to_broadcast([2 * BC, P]), bcr[:, :],
                                          start=True, stop=True).then_inc(s["b_row"], 1)
                            if m < NST - 1:
                                if m:
                                    pe.wait_ge(s["dbu"], n)
                                pe.matmul(ps[:, 5 + (n + 1) % 2, :], sel[:, m + 1:m + 2].to_broadcast([2 * BC, P]),
                                          bcr[:, :], start=True, stop=True).then_inc(s["b_row"], 1)
                            if m:
                                pe.wait_ge(s["hc"], n)
                            pe.matmul(ps[:, 7, :], sel[:, NST + m:NST + m + 1].to_broadcast([2 * BC, P]),
                                      bcr[:, :], start=True, stop=True).then_inc(s["c_row"], 1)
                        elif t == "mix":
                            for m in range(KC):
                                w = slot()
                                for k in range(UC):
                                    i = pe.matmul(ps[:, m, :], w[:, k * P:(k + 1) * P], yg[:, k, :],
                                                  start=(k == 0), stop=(k == UC - 1))
                                i.then_inc(s["mm"], 1)
                        elif t == "t_norm":
                            pe.wait_ge(s["x1"], 4)
                            for k in range(KC):
                                pe.wait_ge(s["sq"], k + 1)
                                i = pe.matmul(ps[:, 0, :], ones, T1[:, k, :], start=(k == 0), stop=(k == KC - 1))
                            i.then_inc(s["stat"], 1)
                        elif t in ("ffn_mm", "exp_mm"):
                            w = slot()
                            f = n if t == "ffn_mm" else FA + n
                            src, g = (T2, 0) if t == "ffn_mm" else (X, 0)
                            b0 = 2 * (f % 2)
                            if t == "ffn_mm" and n < 2:
                                if n == 0:
                                    pe.wait_ge(s["ln"], 1)
                            elif t == "exp_mm" and any(n in (lo, lo + 1) for lo, _ in PASSES):
                                if n < 2:
                                    pe.wait_ge(s["cwr"], 2)
                                    pe.wait_ge(s["x"], 8)
                                else:
                                    p = [lo for lo, _ in PASSES].index(n - n % 2)
                                    pe.wait_ge(s["vpart"], 4 * p)
                            else:
                                pe.wait_ge(s["hid"], f - 1)
                            for g in range(2):
                                for k in range(KC):
                                    if t == "ffn_mm" and n == 0 and g == 0:
                                        pe.wait_ge(s["xn"], k + 1)
                                    o = (g * KC + k) * P
                                    i = pe.matmul(ps[:, b0 + g, :], w[:, o:o + P], src[:, k, :],
                                                  start=(k == 0), stop=(k == KC - 1))
                            i.then_inc(s["gu"], 1)
                        elif t == "exp_ev":
                            if n < ROUTED:
                                if n == 0:
                                    pe.wait_ge(s["cwr"], 2)
                                else:
                                    pe.wait_ge(s["hid"], FA + n)
                                w = (selM[:, MIXED.index(n), :] if n in MIXED
                                     else selE[:, 4 * n:4 * n + 1].to_broadcast([64, P]))
                                pe.matmul(ps[:, 4, :], w, cwr[:, :], start=True, stop=True).then_inc(s["cwb"], 1)
                        elif t == "ffn_down":
                            down(0, FA, 0)
                        elif t == "exp_down":
                            down(*PASSES[n], FA + PASSES[n][0])
                        elif t == "ln_a":
                            for k in range(KC):
                                pe.wait_ge(s["v"], 4 * n + (4 if k == 0 else k + 1))
                                i = pe.matmul(ps[:, 0, :], ones, V[:, k, :], start=(k == 0), stop=(k == KC - 1))
                            i.then_inc(s["mean"], 1)
                        elif t == "ln_b":
                            for k in range(KC):
                                pe.wait_ge(s["sq"], 4 + 4 * n + k + 1 + (4 if n > 2 else 0))
                                i = pe.matmul(ps[:, 1, :], ones, T1[:, k, :], start=(k == 0), stop=(k == KC - 1))
                            i.then_inc(s["stat"], 1)
                        elif t == "gate":
                            pe.wait_ge(s["x"], 4)
                            for e in range(TT):
                                for k in range(KC):
                                    i = pe.transpose(ps[:, e, k * P:(k + 1) * P], X[:, k, e * P:(e + 1) * P], ident)
                                i.then_inc(s["nat"], 1)
                        elif t == "route":
                            pe.wait_ge(s["x"], 8)
                            for e in range(TT):
                                for k in range(KC):
                                    i = pe.matmul(ps[:, 0, e * EXP:(e + 1) * EXP], X[:, k, e * P:(e + 1) * P],
                                                  c("gate", k * EXP, EXP), start=(k == 0), stop=(k == KC - 1))
                            i.then_inc(s["route"], 1)
                            pe.wait_ge(s["cw"], 1)
                            for e in range(TT):
                                i = pe.transpose(ps[0:EXP, 1, e * P:(e + 1) * P], rc[:, e, :], ident)
                            i.then_inc(s["cwt"], 1)
                        elif t == "att_qk":
                            w = slot()
                            pe.wait_ge(s["tctx_in"], 16)
                            pe.wait_ge(s["hid"], FA + FC)
                            for g in range(2):
                                if g:
                                    pe.wait_ge(s["qk_sb"], 1)
                                for k in range(CC):
                                    o = (g * CC + k) * P
                                    i = pe.matmul(ps[:, 4, :], w[:, o:o + P], tcx[:, k, :],
                                                  start=(k == 0), stop=(k == CC - 1))
                                i.then_inc(s["qk"], 1)
                            pe.wait_ge(s["qk_sb"], 2)
                        elif t == "att_row":
                            if n == 0:
                                pe.wait_ge(s["cen"], 12)
                            if n >= 2:
                                pe.wait_ge(s["en_exp"], n - 1)
                            pe.matmul(ps[:, 3 + n % 2, :], qT[:, n * P:(n + 1) * P], kT, start=True, stop=True)\
                                .then_inc(s["en"], 1)
                            if n:
                                turn(n - 1)
                            if n == TT - 1:
                                turn(n)
                        elif t == "seg":
                            pe.wait_ge(s["x"], 12)
                            pe.wait_ge(s["att"], TT)
                            for e in range(TT):
                                for k in range(KC):
                                    i = pe.matmul(ps[:, 2, e * P:(e + 1) * P], X[:, k, e * P:(e + 1) * P],
                                                  wseg[:, k, :], start=(k == 0), stop=(k == KC - 1))
                            i.then_inc(s["score"], 1)
                            pe.wait_ge(s["sq"], 4 + 12 + 4)
                            for e in range(TT):
                                for k in range(KC):
                                    i = pe.matmul(ps[:, 0, e:e + 1], T1[:, k, e * P:(e + 1) * P],
                                                  ones[:, 0:1], start=(k == 0), stop=(k == KC - 1))
                            i.then_inc(s["stat"], 1)
                            pe.wait_ge(s["sg_p"], 1)
                            for e in range(TT):
                                i = pe.transpose(ps[:, 3, e * P:(e + 1) * P], S[:, e * P:(e + 1) * P], ident)
                            i.then_inc(s["att_t"], 1)
                            pe.wait_ge(s["att_sb"], 1)
                            for m in range(KC):
                                pe.matmul(ps[:, m, :], pseg[:, m * P:(m + 1) * P], aT, start=True, stop=True)\
                                    .then_inc(s["down"], 1)
                        elif t == "xmix":
                            pe.wait_ge(s["x"], 16)
                            pe.wait_ge(s["att"], TT)
                            for m in range(KC):
                                for k in range(KC):
                                    i = pe.matmul(ps[:, m, :], att[:, k, m * P:(m + 1) * P], X[:, k, :],
                                                  start=(k == 0), stop=(k == KC - 1))
                                i.then_inc(s["down"], 1)
                        elif t == "bias":
                            pe.wait_ge(s["x"], 20)
                            for e in range(TT):
                                for k in range(KC):
                                    i = pe.matmul(ps[:, 0, e * EXR:(e + 1) * EXR], X[:, k, e * P:(e + 1) * P],
                                                  c("router", k * EXR, EXR), start=(k == 0), stop=(k == KC - 1))
                            i.then_inc(s["route"], 1)
                            for e in range(TT):
                                for k in range(KC):
                                    i = pe.transpose(ps[:, 1 + e, k * P:(k + 1) * P], X[:, k, e * P:(e + 1) * P], ident)
                                i.then_inc(s["nat"], 1)
                            pe.wait_ge(s["wm"], 1)
                            for e in range(TT):
                                i = pe.transpose(ps[0:EXR, 0, e * P:(e + 1) * P], fw[:, e, :], ident)
                            i.then_inc(s["wt_t"], 1)
                            pe.wait_ge(s["wt"], 1)
                            for e in range(TT):
                                pe.wait_ge(s["xs"], e + 1)
                                pe.matmul(ps[:, 1 + e, :], wT[:, e * P:(e + 1) * P], eb[:, :], start=True, stop=True)\
                                    .then_inc(s["down"], 1)

                @block.scalar
                def _(act):
                    cnt = {"ln": 0, "h_ln": 0}

                    def rstd(dst, src, key, eps, parts=P, scale=1.0):
                        pre = "h_" if key == "h" else ""
                        n = cnt[pre + "ln"] = cnt[pre + "ln"] + 1
                        act.preload_act_table_set("natural_log_exp_and_others")
                        act.activation(dst, src, ACT.Ln, bias=c("eps", eps, 1, parts), scale=scale).then_inc(s[pre + "ln"], 1)
                        act.wait_ge(s[pre + "ln"], n)
                        act.activation(dst, dst, ACT.Exp, scale=-0.5).then_inc(s[pre + "rstd"], 1)

                    for t, n in order:
                        if t == "h_norm":
                            if tail:
                                act.wait_ge(s["h_done"], 1)
                            act.dma_start(hx, xT[bass.ds(bh, 1)].rearrange("b p k t -> (b p) k t")).then_inc(s["hx_in"], 16)
                            act.wait_ge(s["hx_in"], 16)
                            for k in range(KC):
                                act.activation(hbv(0)[:, k, :], hx[:, k, :], ACT.Square).then_inc(s["h_sq"], 1)
                            act.wait_ge(s["h_stat"], 1)
                            rstd(hr[:, :], ps[:, 5, :], "h", 0)
                        elif t == "h_proj" and n < UC or t == "h_ctx":
                            k = n + 4 * tail if t == "h_proj" else n
                            act.wait_ge(s["h_mm"], k + 1)
                            act.wait_ge(s["pads"], 1 + tail if t == "h_proj" else 1)
                            if n >= 2:
                                act.wait_ge(s["h_conv"], k - 1)
                            act.activation(up[:, n % 2, 3:], ps[:, 5 + n % 3, :], ACT.Copy).then_inc(s["h_up"], 1)
                            act.wait_ge(s["h_conv"], k + 1)
                            if n >= 2:
                                act.wait_ge(s["h_u"], k - 1)
                            act.activation(ht[:, n % 2, :], cv[:, n % 2, :], ACT.Tanh).then_inc(s["h_th"], 1)
                        elif t == "h_proj":
                            g = n - UC
                            act.wait_ge(s["h_mm"], 4 * tail + n + 1)
                            if g < 2:
                                act.wait_ge(s["h_u"], 4 * tail + UC - 1 + g)
                            else:
                                act.wait_ge(s["h_gz"], g - 1)
                            act.activation(ht[:, n % 2, :], ps[:, 5 + n % 3, :], ACT.Tanh, scale=0.5).then_inc(s["h_th"], 1)
                        elif t == "h_bc":
                            act.wait_ge(s["h_tr"], 2 * tail + 1)
                            act.activation(tn[:, :], ps[:, 5, :], ACT.Square).then_inc(s["h_bsq"], 1)
                            act.wait_ge(s["h_tr"], 2 * tail + 2)
                            act.activation(bcf[:, :], ps[0:BC, 6, :], ACT.Square).then_inc(s["h_bsq"], 1)
                            act.wait_ge(s["h_tstat"], 1)
                            rstd(hr[:, :], ps[:, 7, :], "h", 0, scale=float(HID) / RANK)
                            act.wait_ge(s["h_bstat"], 1)
                            act.wait_ge(s["h_tn"], tail + 1)
                            rstd(hr[0:BC, :], ps[0:BC, 5, :], "h", 0, parts=BC)
                        elif t == "h_dt":
                            act.preload_act_table_set("natural_log_exp_and_others")
                            if n:
                                act.wait_ge(s["h_done"], n)
                            a = n - tail
                            for k in range(4):
                                b = c("dt_bA", 4 * a + k) if a >= 0 else c("dt_bB", k)
                                act.wait_ge(s["h_dtm"], 4 * n + k + 1)
                                act.activation(dl[:, k, :], ps[:, 5 + k % 3, :], ACT.Relu, bias=b)
                                act.activation(hbv(0)[:, k, :], ps[:, 5 + k % 3, :], ACT.Abs, bias=b).then_inc(s["dt_abs"], 1)
                            act.wait_ge(s["dt_abs"], 4 * n + 4)
                            act.activation(hb[:, 0, :], hb[:, 0, :], ACT.Exp, scale=-1.0).then_inc(s["dt_exp"], 1)
                            act.wait_ge(s["dt_one"], n + 1)
                            act.activation(da[:, 0, :], hb[:, 1, :], ACT.Ln).then_inc(s["dt_log"], 1)
                        elif t == "h_scan":
                            u, m = divmod(n, NST)
                            if m == 0:
                                act.wait_ge(s["delta"], u + 1)
                                act.wait_ge(s["firsts"], u + 1)
                            if m >= 2:
                                act.wait_ge(s["scan"], n - 1)
                            for k in range(4):
                                i = act.activation(dav(n % 2)[:, k, 1:], dl[:, k, 1:], ACT.Exp,
                                                   scale=Aneg[:, (4 * (u - tail) if u >= tail else UC) + k, m:m + 1])
                            i.then_inc(s["da"], 1)
                        elif t == "t_norm":
                            for k in range(KC):
                                act.wait_ge(s["x1"], k + 1)
                                act.activation(T1[:, k, :], V[:, k, :], ACT.Square).then_inc(s["sq"], 1)
                            act.wait_ge(s["stat"], 1)
                            rstd(R[:, :], ps[:, 0, :], "t", 0)
                        elif t in ("ffn_ev", "exp_ev"):
                            f = n if t == "ffn_ev" else FA + n
                            act.wait_ge(s["gu"], f + 1)
                            if f >= 2:
                                act.wait_ge(s["hid"], f - 1)
                            act.activation(th[:, f % 2, :], ps[:, 2 * (f % 2), :], ACT.Tanh, scale=0.5)\
                                .then_inc(s["th"], 1)
                        elif t == "ln_a":
                            for k in range(KC):
                                act.wait_ge(s["cen"], 4 * n + k + 1)
                                act.activation(T1[:, k, :], V[:, k, :], ACT.Square).then_inc(s["sq"], 1)
                        elif t == "ln_b":
                            act.wait_ge(s["stat"], n + 2 + (1 if n > 2 else 0))
                            rstd(R[:, :], ps[:, 1, :], "t", 1)
                        elif t == "gate":
                            for e in range(TT):
                                act.wait_ge(s["nat"], e + 1)
                                act.activation(T1[:, e, :], ps[:, e, :], ACT.Tanh, scale=0.5).then_inc(s["gz"], 1)
                        elif t == "route":
                            act.wait_ge(s["rt"], 2)
                            act.activation(re[:, :, :], re[:, :, :], ACT.Exp).then_inc(s["rexp"], 1)
                        elif t == "att_qk":
                            act.wait_ge(s["down"], 4 * (1 + len(PASSES)))
                            act.dma_start(tcx, ctxT[bass.ds(bt, 1)].rearrange("b p k t -> (b p) k t")).then_inc(s["tctx_in"], 16)
                            for g, (dst, b) in enumerate(((qT, "bq"), (kT, "bk"))):
                                act.wait_ge(s["qk"], g + 1)
                                act.activation(dst, ps[:, 4, :], ACT.Identity, bias=c(b)).then_inc(s["qk_sb"], 1)
                        elif t == "att_row":
                            act.wait_ge(s["en_max"], n + 1)
                            if n >= 2:
                                act.wait_ge(s["en_t"], n - 1)
                            act.activation(erow(n), ps[:, 3 + n % 2, :], ACT.Exp, bias=nmax[:, n:n + 1],
                                           accum_out=esum[:, n:n + 1]).then_inc(s["en_exp"], 1)
                            for m in ([n - 1] if n else []) + ([n] if n == TT - 1 else []):
                                act.wait_ge(s["en_t"], m + 1)
                                act.activation(att[:, :, m * P:(m + 1) * P],
                                               ps[:, 2, :].rearrange("p (k m) -> p k m", m=P), ACT.Copy)\
                                    .then_inc(s["att"], 1)
                        elif t == "seg":
                            act.wait_ge(s["x"], 12)
                            for k in range(KC):
                                act.activation(T1[:, k, :], X[:, k, :], ACT.Square).then_inc(s["sq"], 1)
                            act.wait_ge(s["stat"], 5)
                            rstd(r4, ps[:, 0, 0:TT], "t", 2)
                            act.wait_ge(s["sg_s"], 3)
                            act.activation(S, S, ACT.Exp).then_inc(s["seg_exp"], 1)
                            act.wait_ge(s["att_t"], 1)
                            act.activation(aT, ps[:, 3, :], ACT.Copy).then_inc(s["att_sb"], 1)
                        elif t == "bias":
                            act.wait_ge(s["ft"], 3)
                            act.activation(fl[:, :, :], fl[:, :, :], ACT.Exp).then_inc(s["fexp"], 1)
                            act.wait_ge(s["wm"], 2)
                            for e in range(TT):
                                act.wait_ge(s["nat"], TT + e + 1)
                                act.activation(T1[:, e, :], ps[:, 1 + e, :], ACT.Copy, scale=rs[:, e:e + 1])\
                                    .then_inc(s["xs"], 1)
                            act.wait_ge(s["bn"], 2)
                            rstd(r4, mv[:, :, 1], "t", 1)

                @block.vector
                def _(dve):
                    vt = [0]

                    def center(n):
                        dve.wait_ge(s["mean"], n + 1)
                        for k in range(KC):
                            dve.tensor_tensor(V[:, k, :], V[:, k, :], ps[:, 0, :], ALU.subtract).then_inc(s["cen"], 1)

                    def evac_sum(base, v0, src, last):
                        for m in range(KC):
                            dve.wait_ge(s["down"], base + m + 1)
                            dve.tensor_tensor(V[:, m, :], ps[:, m, :], src[:, m, :], ALU.add)\
                                .then_inc(s["v" if last else "vpart"], 1)

                    taps = [0]

                    def conv(k, n, w, b):
                        dve.wait_ge(s["h_up"], k + 1)
                        if n >= 2:
                            dve.wait_ge(s["h_u"], k - 1)
                        dve.tensor_scalar(cv[:, n % 2, :], up[:, n % 2, 3:], c(w, n * TAPS + 3), c(b, n),
                                          ALU.mult, ALU.add).then_inc(s["h_tap"], 1)
                        taps[0] += 1
                        for tap in range(3):
                            dve.wait_ge(s["h_tap"], taps[0])
                            i = dve.scalar_tensor_tensor(out=cv[:, n % 2, :], in0=up[:, n % 2, tap:tap + TOK],
                                                         scalar=c(w, n * TAPS + tap), in1=cv[:, n % 2, :],
                                                         op0=ALU.mult, op1=ALU.add)
                            if tap < 2:
                                i.then_inc(s["h_tap"], 1)
                                taps[0] += 1
                            else:
                                i.then_inc(s["h_conv"], 1)

                    def silu(k, n, seen):
                        dve.wait_ge(s["h_th"], seen)
                        dve.scalar_tensor_tensor(out=ucv[:, n, :], in0=ht[:, n % 2, :], scalar=1.0,
                                                 in1=cv[:, n % 2, :], op0=ALU.add, op1=ALU.mult).then_inc(s["h_u"], 1)

                    for t, n in order:
                        if t == "h_norm":
                            dve.wait_ge(s["h_rstd"], 1)
                            for k in range(KC):
                                dve.scalar_tensor_tensor(out=hx[:, k, :], in0=hx[:, k, :], scalar=c("in_ln", k),
                                                         in1=hr[:, :], op0=ALU.mult, op1=ALU.mult).then_inc(s["h_xn"], 1)
                        elif t == "h_proj" and n < UC:
                            conv(4 * tail + n, n, "conv_wA", "conv_bA")
                            silu(4 * tail + n, n, 4 * tail + n + 1)
                        elif t == "h_proj":
                            g = n - UC
                            dve.wait_ge(s["h_th"], 4 * tail + n + 1)
                            if tail and g == 0:
                                dve.wait_ge(s["mm"], 4)
                            dve.scalar_tensor_tensor(out=yg[:, g, :], in0=ht[:, n % 2, :], scalar=1.0,
                                                     in1=ps[:, 5 + n % 3, :], op0=ALU.add, op1=ALU.mult)\
                                .then_inc(s["h_gz"], 1)
                        elif t == "h_bc":
                            dve.wait_ge(s["h_rstd"], 2)
                            dve.scalar_tensor_tensor(out=tn[:, :], in0=ps[:, 5, :], scalar=c("dt_ln"), in1=hr[:, :],
                                                     op0=ALU.mult, op1=ALU.mult).then_inc(s["h_tn"], 1)
                            dve.wait_ge(s["h_rstd"], 3)
                            dve.scalar_tensor_tensor(out=bcf[:, :], in0=ps[0:BC, 6, :], scalar=c("bc_ln", 0, 1, BC),
                                                     in1=hr[0:BC, :], op0=ALU.mult, op1=ALU.mult).then_inc(s["h_bcf"], 1)
                            dve.wait_ge(s["h_bcf"], 1)
                            dve.tensor_copy(bcr[0:BC, :], bcf[:, :]).then_inc(s["h_bc"], 1)
                            dve.wait_ge(s["h_bc"], 2 * tail + 1)
                            dve.tensor_tensor(bcr[BC:2 * BC, :], bcf[:, :], bcr[0:BC, :].bitcast(f32), ALU.subtract)\
                                .then_inc(s["h_bc"], 1)
                        elif t == "h_ctx":
                            conv(n, n, "conv_wB", "conv_bB")
                            silu(n, n, n + 1)
                        elif t == "h_ctxbc":
                            dve.wait_ge(s["h_tr"], 1)
                            dve.tensor_copy(tn[0:RANKB, :], ps[0:RANKB, 5, :]).then_inc(s["h_tn"], 1)
                            dve.wait_ge(s["h_tr"], 2)
                            dve.tensor_copy(bcr[0:BC, :], ps[0:BC, 6, :]).then_inc(s["h_bc"], 1)
                            dve.wait_ge(s["h_bc"], 1)
                            dve.tensor_tensor(bcr[BC:2 * BC, :], ps[0:BC, 6, :], bcr[0:BC, :].bitcast(f32), ALU.subtract)\
                                .then_inc(s["h_bc"], 1)
                        elif t == "h_dt":
                            dve.wait_ge(s["dt_exp"], n + 1)
                            dve.tensor_scalar(hb[:, 1, :], hb[:, 0, :], 1.0, None, ALU.add).then_inc(s["dt_one"], 1)
                            dve.wait_ge(s["dt_log"], n + 1)
                            dve.scalar_tensor_tensor(out=hb[:, 1, :], in0=hb[:, 1, :], scalar=-1.0, in1=hb[:, 0, :],
                                                     op0=ALU.add, op1=ALU.subtract).then_inc(s["dt_res"], 1)
                            dlf = dl[:, :, :].rearrange("p c t -> p (c t)")
                            dve.wait_ge(s["dt_res"], 3 * n + 1)
                            dve.tensor_tensor(hb[:, 1, :], da[:, 0, :], hb[:, 1, :], ALU.subtract).then_inc(s["dt_res"], 1)
                            dve.wait_ge(s["dt_res"], 3 * n + 2)
                            dve.tensor_tensor(dlf, dlf, hb[:, 1, :], ALU.add).then_inc(s["dt_res"], 1)
                            dve.wait_ge(s["dt_res"], 3 * n + 3)
                            a = max(n - tail, 0)
                            uu = ucv[:, 4 * a:4 * a + 4, :]
                            dve.tensor_tensor(du[:, :, :], dl[:, :, :], uu, ALU.mult).then_inc(s["delta"], 1)
                        elif t == "h_scan":
                            u, m = divmod(n, NST)
                            dve.wait_ge(s["b_row"], n + 1)
                            dve.wait_ge(s["delta"], u + 1)
                            if m >= 2:
                                dve.wait_ge(s["acc"], n - 1)
                            dve.tensor_tensor(hbv(n % 2), du[:, :, :], wide(ps[:, 5 + n % 2, :], 4), ALU.mult)\
                                .then_inc(s["dbu"], 1)
                            dve.wait_ge(s["da"], n + 1)
                            dve.wait_ge(s["dbu"], n + 1)
                            dve.tensor_tensor_scan(hb[:, n % 2, :], da[:, n % 2, :], hb[:, n % 2, :], 0.0,
                                                   ALU.mult, ALU.add).then_inc(s["scan"], 1)
                            dve.wait_ge(s["c_row"], n + 1)
                            dve.wait_ge(s["scan"], n + 1)
                            dve.tensor_tensor(hbv(n % 2), hbv(n % 2), wide(ps[:, 7, :], 4), ALU.mult)\
                                .then_inc(s["hc"], 1)
                        elif t == "h_fin":
                            dve.wait_ge(s["acc"], NST * (n + 1))
                            a = n - tail
                            for k in range(4):
                                dst = hbv(0)[:, k, :] if a >= 0 else yb[:, k, :]
                                i = dve.scalar_tensor_tensor(out=dst, in0=ucv[:, 4 * max(a, 0) + k, :],
                                                             scalar=c("DA", 4 * a + k) if a >= 0 else c("DB", k),
                                                             in1=ya[:, k, :], op0=ALU.mult, op1=ALU.add)
                            if a < 0:
                                i.then_inc(s["h_done"], 1)
                            else:
                                i.then_inc(s["h_y"], 1)
                                dve.wait_ge(s["h_y"], a + 1)
                                dve.scalar_tensor_tensor(out=yg[:, 4 * a:4 * a + 4, :], in0=hbv(0), scalar=0.5,
                                                         in1=yg[:, 4 * a:4 * a + 4, :], op0=ALU.mult, op1=ALU.mult)\
                                    .then_inc(s["h_done"], 1)
                        elif t == "mix":
                            dve.wait_ge(s["x_in"], 16)
                            for m in range(KC):
                                dve.wait_ge(s["mm"], m + 1)
                                dve.tensor_tensor(V[:, m, :], ps[:, m, :], X[:, m, :], ALU.add).then_inc(s["x1"], 1)
                        elif t == "t_norm":
                            dve.wait_ge(s["rstd"], 1)
                            for k in range(KC):
                                dve.scalar_tensor_tensor(out=T2[:, k, :], in0=V[:, k, :], scalar=c("pre_ln", k),
                                                         in1=R[:, :], op0=ALU.mult, op1=ALU.mult).then_inc(s["xn"], 1)
                        elif t in ("ffn_ev", "exp_ev"):
                            f = n if t == "ffn_ev" else FA + n
                            lo = 0 if t == "ffn_ev" else max(a for a, _ in PASSES if a <= n)
                            b0 = 2 * (f % 2)
                            dve.wait_ge(s["th"], f + 1)
                            dve.scalar_tensor_tensor(out=th[:, f % 2, :], in0=th[:, f % 2, :], scalar=1.0,
                                                     in1=ps[:, b0, :], op0=ALU.add, op1=ALU.mult).then_inc(s["sg"], 1)
                            dve.wait_ge(s["sg"], f + 1)
                            if t == "exp_ev" and n == lo:
                                dve.wait_ge(s["down"], 4 * (1 + [a for a, _ in PASSES].index(lo)))
                            plain = t == "ffn_ev" or n >= ROUTED
                            dst = hid[:, n - lo, :]
                            dve.scalar_tensor_tensor(out=dst, in0=th[:, f % 2, :], scalar=0.5, in1=ps[:, b0 + 1, :],
                                                     op0=ALU.mult, op1=ALU.mult)\
                                .then_inc(s["hid" if plain else "su"], 1)
                            if not plain:
                                dve.wait_ge(s["su"], n + 1)
                                dve.wait_ge(s["cwb"], n + 1)
                                dve.tensor_tensor(dst, dst, ps[:, 4, :], ALU.mult).then_inc(s["hid"], 1)
                        elif t == "ffn_down":
                            dve.wait_ge(s["resid"], 1)
                            evac_sum(0, 0, X, True)
                        elif t == "exp_down":
                            if n:
                                dve.wait_ge(s["vpart"], 4 * n)
                            evac_sum(4 * (n + 1), 8, V if n else X, n == len(PASSES) - 1)
                        elif t == "ln_a":
                            center(n)
                        elif t == "ln_b":
                            dve.wait_ge(s["rstd"], n + 2 + (1 if n > 2 else 0))
                            for k in range(KC):
                                dve.tensor_tensor(X[:, k, :], V[:, k, :], R[:, :], ALU.mult).then_inc(s["x"], 1)
                        elif t == "gate":
                            for e in range(TT):
                                dve.wait_ge(s["gz"], e + 1)
                                dve.scalar_tensor_tensor(out=T2[:, e, :], in0=T1[:, e, :], scalar=1.0, in1=ps[:, e, :],
                                                         op0=ALU.add, op1=ALU.mult).then_inc(s["g1"], 1)
                                dve.wait_ge(s["g1"], e + 1)
                                dve.scalar_tensor_tensor(out=T2[:, e, :], in0=T2[:, e, :], scalar=0.5, in1=yb[:, e, :],
                                                         op0=ALU.mult, op1=ALU.mult).then_inc(s["g2"], 1)
                                dve.wait_ge(s["g2"], e + 1)
                                dve.tensor_tensor(V[:, e, :], T2[:, e, :], X[:, e, :], ALU.add).then_inc(s["v"], 1)
                        elif t == "route":
                            pr = ps[:, 0, 0:TT * EXP].rearrange("p (t e) -> p t e", e=EXP)
                            k = [0]

                            def step(i):
                                k[0] += 1
                                i.then_inc(s["rt"], 1)
                                dve.wait_ge(s["rt"], k[0])

                            dve.wait_ge(s["route"], 1)
                            for e in range(TT):
                                i = dve.max(rm[:, e, :], pr[:, e, :])
                            step(i)
                            step(dve.tensor_tensor(re[:, :, :], pr, rm[:, :, 0:1].to_broadcast([P, TT, EXP]), ALU.subtract))
                            dve.wait_ge(s["rexp"], 1)
                            step(dve.tensor_reduce(rs, re[:, :, :], AX.X, ALU.add))
                            step(dve.reciprocal(rs, rs))
                            step(dve.tensor_tensor(rp[:, :, :], re[:, :, :], rs.unsqueeze(2).to_broadcast([P, TT, EXP]), ALU.mult))
                            for e in range(TT):
                                i = dve.max(rm[:, e, :], rp[:, e, :])
                            step(i)
                            for e in range(TT):
                                i = dve.max_index(ri[:, e, :], rm[:, e, :], rp[:, e, :])
                            step(i)
                            step(dve.tensor_copy(rf[:, :, :], ri[:, :, :]))
                            step(dve.scalar_tensor_tensor(out=rs, in0=rm[:, :, 0], scalar=1e-20, in1=rm[:, :, 1],
                                                          op0=ALU.add, op1=ALU.add))
                            step(dve.reciprocal(rs, rs))
                            step(dve.tensor_tensor(rw[:, :, :], rm[:, :, 0:2], rs.unsqueeze(2).to_broadcast([P, TT, 2]), ALU.mult))
                            for e in range(TT):
                                dve.tensor_scalar(ra[:, e, :], c("iota", 0, EXP), rf[:, e, 0:1], rw[:, e, 0:1],
                                                  ALU.is_equal, ALU.mult)
                                i = dve.tensor_scalar(rb[:, e, :], c("iota", 0, EXP), rf[:, e, 1:2], rw[:, e, 1:2],
                                                      ALU.is_equal, ALU.mult)
                            step(i)
                            dve.tensor_tensor(rc[:, :, :], ra[:, :, :], rb[:, :, :], ALU.add).then_inc(s["cw"], 1)
                            dve.wait_ge(s["cwt"], 1)
                            dve.tensor_copy(cwr[0:EXP, :], ps[0:EXP, 1, :]).then_inc(s["cwr"], 1)
                            dve.wait_ge(s["cwr"], 1)
                            dve.tensor_tensor(cwr[32:32 + EXP, :], ps[0:EXP, 1, :], cwr[0:EXP, :].bitcast(f32),
                                              ALU.subtract).then_inc(s["cwr"], 1)
                        elif t == "att_row":
                            dve.wait_ge(s["en"], n + 1)
                            dve.tensor_reduce(nmax[:, n:n + 1], ps[:, 3 + n % 2, :], AX.X, ALU.max, negate=True)\
                                .then_inc(s["en_max"], 1)
                            dve.wait_ge(s["en_exp"], n + 1)
                            dve.reciprocal(esum[:, n:n + 1], esum[:, n:n + 1]).then_inc(s["en_rec"], 1)
                        elif t == "seg":
                            dve.wait_ge(s["score"], 1)
                            dve.wait_ge(s["rstd"], 5)
                            S3 = S.rearrange("p (t h j) -> p t h j", h=HEADS, j=SEG)
                            Sj = S.rearrange("p (h j) -> p h j", j=SEG)
                            for e in range(TT):
                                i = dve.scalar_tensor_tensor(
                                    out=S3[:, e], in0=ps[:, 2, e * P:(e + 1) * P].rearrange("p (h j) -> p h j", j=SEG),
                                    scalar=r4[:, e:e + 1], in1=wide(c("mask", 0, SEG), HEADS), op0=ALU.mult, op1=ALU.add)
                            i.then_inc(s["sg_s"], 1)
                            dve.wait_ge(s["sg_s"], 1)
                            dve.tensor_reduce(smx[:, :], Sj, AX.X, ALU.max).then_inc(s["sg_s"], 1)
                            dve.wait_ge(s["sg_s"], 2)
                            mb = smx[:, :].unsqueeze(2).to_broadcast([P, P, SEG])
                            dve.tensor_tensor(Sj, Sj, mb, ALU.subtract).then_inc(s["sg_s"], 1)
                            dve.wait_ge(s["seg_exp"], 1)
                            dve.tensor_reduce(smx[:, :], Sj, AX.X, ALU.add).then_inc(s["sg_s"], 1)
                            dve.wait_ge(s["sg_s"], 4)
                            dve.reciprocal(smx[:, :], smx[:, :]).then_inc(s["sg_s"], 1)
                            dve.wait_ge(s["sg_s"], 5)
                            dve.tensor_tensor(Sj, Sj, mb, ALU.mult).then_inc(s["sg_p"], 1)
                            evac_sum(16, 12, X, True)
                        elif t == "xmix":
                            for m in range(KC):
                                dve.wait_ge(s["down"], 20 + m + 1)
                                dve.wait_ge(s["en_rec"], TT)
                                dve.scalar_tensor_tensor(out=V[:, m, :], in0=ps[:, m, :], scalar=esum[:, m:m + 1],
                                                         in1=X[:, m, :], op0=ALU.mult, op1=ALU.add).then_inc(s["v"], 1)
                        elif t == "bias":
                            pf = ps[:, 0, 0:TT * EXR].rearrange("p (t e) -> p t e", e=EXR)
                            k = [0]

                            def fstep(i):
                                k[0] += 1
                                i.then_inc(s["ft"], 1)
                                dve.wait_ge(s["ft"], k[0])

                            dve.wait_ge(s["route"], 2)
                            fstep(dve.tensor_tensor(fl[:, :, :], pf, wide(c("rbias", 0, EXR), TT), ALU.add))
                            for e in range(TT):
                                i = dve.max(rm[:, e, :], fl[:, e, :])
                            fstep(i)
                            fstep(dve.tensor_tensor(fl[:, :, :], fl[:, :, :], rm[:, :, 0:1].to_broadcast([P, TT, EXR]), ALU.subtract))
                            dve.wait_ge(s["fexp"], 1)
                            fstep(dve.tensor_reduce(rs, fl[:, :, :], AX.X, ALU.add))
                            fstep(dve.reciprocal(rs, rs))
                            fstep(dve.tensor_tensor(fl[:, :, :], fl[:, :, :], rs.unsqueeze(2).to_broadcast([P, TT, EXR]), ALU.mult))
                            for e in range(TT):
                                i = dve.max(rm[:, e, :], fl[:, e, :])
                            fstep(i)
                            for e in range(TT):
                                i = dve.match_replace(fr[:, e, :], rm[:, e, :], fl[:, e, :], 0.0)
                            fstep(i)
                            dve.tensor_tensor(fw[:, :, :], fl[:, :, :], fr[:, :, :], ALU.subtract).then_inc(s["wm"], 1)
                            fstep(dve.tensor_reduce(rs, rm[:, :, :], AX.X, ALU.add))
                            dve.tensor_scalar(rs, rs, 1.0, None, ALU.add).then_inc(s["wm"], 1)
                            dve.wait_ge(s["wt_t"], 1)
                            dve.tensor_copy(wT, ps[0:EXR, 0, :]).then_inc(s["wt"], 1)
                            for e in range(TT):
                                dve.wait_ge(s["down"], 24 + e + 1)
                                fstep(dve.tensor_tensor(V[:, e, :], ps[:, 1 + e, :], T1[:, e, :], ALU.add))
                                i = dve.bn_stats(bn[:, e, :], V[:, e, :])
                            i.then_inc(s["bn"], 1)
                            dve.wait_ge(s["bn"], 1)
                            for e in range(TT):
                                i = dve.bn_aggr(mv[:, e, :], bn[:, e, :])
                            i.then_inc(s["bn"], 1)
                            dve.wait_ge(s["rstd"], 8)
                            for e in range(TT):
                                dve.tensor_scalar(V[:, e, :], V[:, e, :], mv[:, e, 0:1], r4[:, e:e + 1],
                                                  ALU.subtract, ALU.mult).then_inc(s["y"], 1)

                @block.gpsimd
                def _(pool):
                    pool.memset(up[:, :, 0:3], 0.0).then_inc(s["pads"], 1)
                    for t, n in order:
                        if t == "t_norm":
                            pool.wait_ge(s["x1"], 4)
                            pool.tensor_tensor(X[:, :, :], X[:, :, :], V[:, :, :], ALU.add).then_inc(s["resid"], 1)
                        elif t == "h_norm" and tail:
                            pool.wait_ge(s["h_done"], 1)
                            pool.memset(up[:, :, 0:3], 0.0).then_inc(s["pads"], 1)
                        elif t == "h_scan":
                            u, m = divmod(n, NST)
                            if m == 0:
                                pool.wait_ge(s["delta"], u + 1)
                                pool.memset(da[:, :, :].rearrange("p i (c t) -> p (i c) t", t=TOK)[:, :, 0:1], 0.0)\
                                    .then_inc(s["firsts"], 1)
                            pool.wait_ge(s["hc"], n + 1)
                            if m == 0:
                                if u:
                                    pool.wait_ge(s["h_done"], u)
                                pool.tensor_copy(ya[:, :, :], hbv(n % 2)).then_inc(s["acc"], 1)
                            else:
                                pool.wait_ge(s["acc"], n)
                                pool.tensor_tensor(ya[:, :, :], ya[:, :, :], hbv(n % 2), ALU.add).then_inc(s["acc"], 1)
            nc.all_engine_barrier(sems_to_clear=every)

        run(0, None)
        with nc.Fori(0, SEQS - 1) as b:
            run(b + 1, b)
        run(None, SEQS - 1)


def kernel(**inputs):
    import numpy as np
    import concourse.bacc as _bacc
    from concourse import mybir as _mybir
    from concourse.bass_utils import run_bass_kernel_spmd as _run

    g = {k: np.asarray(v) for k, v in inputs.items()}
    f = np.float32

    def cols(v, n):
        v = v.reshape((n, P) + v.shape[1:])
        return np.moveaxis(v, 0, 1).reshape(P, -1)

    def tiles(w, mc, kc):
        return np.ascontiguousarray(w.reshape(mc, P, kc, P).transpose(0, 3, 2, 1)).reshape(mc, P, kc * P)

    pack = np.zeros((P, PACK), f)

    def put(name, v):
        v = v.reshape(v.shape[0], -1)
        pack[:v.shape[0], COL[name]:COL[name] + v.shape[1]] = v

    A, B, M, D, E, F = "L0_attn_", "L0_xattn_", "L0_ffn_", "L1_attn_", "L1_xattn_", "L1_ffn_"
    put("in_ln", cols(g[A + "input_ln_w"], KC))
    put("pre_ln", cols(g[A + "pre_ff_ln_w"], KC))
    put("conv_bA", cols(g[A + "conv_b"], UC))
    put("conv_wA", cols(g[A + "conv_w"].reshape(DI, TAPS), UC))
    put("dt_bA", cols(g[A + "b_dt"], UC))
    put("DA", cols(g[A + "D_skip"], UC))
    put("A_logA", cols(g[A + "A_log"], UC))
    put("dt_ln", g[A + "dt_ln_w"])
    put("bc_ln", np.concatenate([g[A + "b_ln_w"], g[A + "c_ln_w"]]))
    put("conv_bB", cols(g[B + "conv_b"], 4))
    put("conv_wB", cols(g[B + "conv_w"], 4))
    put("dt_bB", cols(g[B + "dt_proj_b"], 4))
    put("DB", cols(g[B + "D"], 4))
    put("A_logB", cols(g[B + "A_log"], 4))
    put("seg_ln", cols(g[D + "w_norm"], KC))
    put("bq", g[E + "bq"])
    put("bk", g[E + "bk"])
    put("eps", np.broadcast_to(np.array([EPS, EPS_LN, EPS_SEG], f), (P, 3)))
    put("mask", np.where(np.arange(SEG)[None] <= np.arange(P)[:, None] % SEG, 0, NEG).astype(f))
    put("iota", np.broadcast_to(np.arange(EXP, dtype=f), (P, EXP)))
    put("blk", (np.arange(BC)[:, None] // NST == np.arange(BC)[None] // NST).astype(f) / NST)
    rows = np.arange(64)
    put("group", ((rows[:, None] % 32 == np.arange(FC * 4)[None] // (FE // 32)) & (rows[:, None] % 32 < EXP)).astype(f))
    put("ident", np.eye(P, dtype=f))
    put("gate", cols(np.ascontiguousarray(g[M + "gate_weight"].T), KC))
    put("router", cols(np.ascontiguousarray(g[F + "router_weight"].T), KC))
    put("rbias", np.broadcast_to(g[F + "router_bias"], (P, EXR)))
    put("ones", np.full((P, P), 1.0 / HID, f))

    fe = EXP * FE + FS
    up_all = np.zeros((2, FC * P, HID), f)
    up_all[0, :fe] = np.concatenate([g[M + "w_gate"].reshape(-1, HID), g[M + "sw_gate"]])
    up_all[1, :fe] = np.concatenate([g[M + "w_up"].reshape(-1, HID), g[M + "sw_up"]])
    dn_all = np.zeros((FC * P, HID), f)
    dn_all[:fe] = np.concatenate([g[M + "w_down"].transpose(0, 2, 1).reshape(-1, HID), g[M + "sw_down"].T])
    w_x = g[A + "w_x"]
    arrays = {
        "pack": pack,
        "w_in": tiles(g[A + "w_in"], 16, KC).reshape(8, 2, P, KC * P).transpose(0, 2, 1, 3).reshape(8, P, SLOT),
        "w_x": tiles(w_x[:RANK], 1, UC)[0],
        "w_bc": cols(np.ascontiguousarray(w_x[RANK:].T), UC),
        "w_dt": g[A + "w_dt"].T,
        "x_in_w": tiles(g[B + "in_proj_w"], 4, CC).transpose(1, 0, 2).reshape(P, SLOT),
        "x_proj_w": cols(np.ascontiguousarray(g[B + "x_proj_w"].T), 4),
        "x_dt_w": g[B + "dt_proj_w"].T,
        "w_out": tiles(g[A + "w_out"], KC, UC),
        "w_fgu": np.concatenate([tiles(g[A + "w_gate"], FA, KC), tiles(g[A + "w_up"], FA, KC)], axis=2),
        "w_fdn": g[A + "w_down"].T.reshape(FA, P, HID),
        "w_egu": np.concatenate([tiles(up_all[0], FC, KC), tiles(up_all[1], FC, KC)], axis=2),
        "w_edn": dn_all.reshape(FC, P, HID),
        "w_qk": np.concatenate([tiles(g[E + "Wq"], 1, CC)[0], tiles(g[E + "Wk"], 1, CC)[0]], axis=1),
        "ebias": g[F + "expert_bias"],
        "wq_t": g[D + "w_qkv"][:, :HEADS * DH].T.reshape(16, P, HID),
        "wo": g[D + "w_out"].reshape(16, P, HID),
        "pm": g[D + "pm"].reshape(2, 16, 2, 16, DH).transpose(0, 2, 4, 1, 3).reshape(2, P, 16, 16),
        "xT": g["x"].transpose(0, 2, 1).reshape(SEQS, KC, P, TOK).transpose(0, 2, 1, 3),
        "ctxT": g["ctx_1024"].transpose(0, 2, 1).reshape(SEQS, CC, P, TOK).transpose(0, 2, 1, 3),
    }
    nc = _bacc.Bacc("TRN2", target_bir_lowering=False, num_devices=1)
    feeds, args = {}, []
    for name, a in arrays.items():
        a = np.ascontiguousarray(a)
        feeds["in_" + name] = a
        args.append(nc.dram_tensor("in_" + name, a.shape, _mybir.dt.from_np(a.dtype), kind="ExternalInput").ap())
    args.append(nc.dram_tensor("out", (SEQS, TOK, HID), _mybir.dt.float32, kind="ExternalOutput").ap())
    build(nc, *args)
    r = _run(nc, [feeds], core_ids=[0])
    return r.results[0]["out"]
```

```python
import concourse.bass as bass
from concourse import mybir
from contextlib import ExitStack

P = 128
SEQS, TOK, HID = 4, 512, 512
KC = HID // P
TT = TOK // P
DI, NST, RANK, TAPS = 1024, 16, 128, 4
UC = DI // P
CTX, DIB, RANKB = 256, 512, 16
CC = CTX // P
ROWSB = 64
FF = 1408
FA = FF // P
EXP, FE, FS = 8, 352, 704
SHARED = -(-FS // P)
ROUTED = EXP * FE // P
FC = SHARED + ROUTED
MIXED = [c for c in range(ROUTED) if c * P // FE != (c * P + P - 1) // FE]
PASSES = [(0, 8), (8, 18), (18, FC)]
HIDMAX = FA
POOLED = 1
HEADS, DH, SEG = 32, 64, 4
FOLDS = HEADS * DH // P
EXR = 64
NSLOT, SLOT = 7, 1024
BC = 2 * NST
EPS, EPS_LN = 1e-6, 1e-5
EPS_SEG = 1.1920929e-07
NEG = -3.0e38

_PACK = [("in_ln", KC), ("pre_ln", KC), ("conv_bA", UC), ("conv_wA", UC * TAPS), ("dt_bA", UC),
         ("DA", UC), ("A_logA", UC * NST), ("A_logB", 4 * NST), ("dt_ln", 1), ("bc_ln", 1), ("conv_bB", 4),
         ("conv_wB", 4 * TAPS), ("dt_bB", 4), ("DB", 4), ("seg_ln", KC),
         ("bq", 1), ("bk", 1), ("eps", 3), ("mask", SEG), ("iota", EXP), ("blk", BC),
         ("group", ROUTED * 4), ("ident", P), ("gate", KC * EXP), ("router", KC * EXR), ("rbias", EXR),
         ("ones", P)]
COL = {}
PACK = 0
for _n, _c in _PACK:
    COL[_n] = PACK
    PACK += _c


def unit(q):
    return [("h_dt", q), ("h_dt_b", q), ("h_dt_c", q)] + [("h_scan", NST * q + n) for n in range(NST)] + [("h_fin", q)]


def hidden(kind, chunks):
    out = []
    for c in chunks:
        out.append((kind + "_mm", c))
        if c > chunks[0]:
            out.append((kind + "_ev", c - 1))
    return out + [(kind + "_ev", chunks[-1])]


def span(t, k):
    return (0, FA) if t == "ffn_down" else [x for x in PASSES if x[0] <= k < x[1]][0]


COST = {"h_mix": 7, "h_norm": 8.56, "seg_fold": 1, "seg_folded": 1, "h_proj": 4, "h_ctx": 5,
        "h_ctxbc": 2.25, "h_bc": 11.9, "h_bn": 8.4, "h_dt": 7, "h_dt_b": 5.75, "h_dt_c": 10, "h_scan": 7,
        "h_fin": 4.65, "ffn_mm": 7, "exp_mm": 7, "ffn_down": 9, "exp_down": 9.63, "ln_a": 7, "ln_b": 7,
        "gate": 6, "route_a": 5, "route_b": 5, "route_c": 4, "att_qk": 5, "att_row": 3.79, "seg_a": 7,
        "seg_b": 6, "seg_c": 5, "xmix": 14, "bias_a": 8, "bias_b": 8, "bias_c": 8}


def merge(a, b):
    total_a, total_b = (sum(COST.get(t, 0) for t, _ in x) for x in (a, b))
    out, at_a, at_b, a, b = [], 0.0, 0.0, list(a), list(b)
    while a or b:
        if b and (not a or b[0][0] not in COST or at_b * total_a < at_a * total_b):
            at_b += COST.get(b[0][0], 0)
            out.append(b.pop(0))
        else:
            at_a += COST.get(a[0][0], 0)
            out.append(a.pop(0))
    return out


def schedule(tail, scan, proj):
    scans = unit(tail) + unit(tail + 1) if scan else []
    ahead = [("h_mix", m) for m in range(KC)] if scan else []
    if proj:
        ahead += [("h_norm", 0)] + [("h_proj", j) for j in range(2 * UC)] + [("h_bc", 0), ("h_bn", 0)]
    if not tail:
        folds = [("seg_fold", k) for k in range(FOLDS)] + [("seg_folded", 0)] if scan else []
        return merge(scans, folds) + ahead
    start = [("x1", 0)] + [("h_ctx", j) for j in range(4)] + [("h_ctxbc", 0), ("t_norm", 0), ("h_dt", 0),
             ("h_dt_b", 0)]
    side = unit(0)[2:]
    ffn = hidden("ffn", range(FA)) + [("ffn_down", k) for k in range(0, FA, 2)] + [("ln_a", 0), ("ln_b", 0)]
    experts = [("gate", 0), ("att_qk", 0), ("ln_a", 1), ("att_row", 0), ("att_row", 1), ("ln_b", 1),
               ("att_row", 2), ("att_row", 3)]
    for lo, hi in PASSES:
        experts += hidden("exp", range(lo, hi)) + [("exp_down", k) for k in range(lo, hi, 2)]
    for step, after in (("route_a", 0), ("route_b", 2), ("route_c", 4)):
        experts.insert(experts.index(("exp_mm", after)), (step, 0))
    rest = [("ln_a", 2), ("ln_b", 2), ("seg_a", 0), ("seg_b", 0), ("seg_c", 0), ("ln_a", 3), ("ln_b", 3),
            ("xmix", 0), ("ln_a", 4), ("ln_b", 4), ("bias_a", 0), ("bias_b", 0), ("bias_c", 0)]
    return start + merge(side, ffn) + experts[:1] + merge(scans, experts[1:]) + merge(ahead, rest)


SIGNALS = (
    [f"slot{i}" for i in range(NSLOT)] + ["x_in", "hx_in", "ctx_in", "tctx_in", "out_done"] +
    ["h_stat", "h_mm", "h_tr", "h_tstat", "h_bstat", "h_dtm", "b_row", "c_row",
     "h_sq", "h_ln", "h_rstd", "h_up", "h_th", "h_bsq", "dt_abs", "dt_exp", "dt_log", "da",
     "h_xn", "h_tap", "h_conv", "h_u", "h_gz", "h_tn", "h_bcf", "h_bc", "dt_one", "dt_res", "delta",
     "dbu", "scan", "hc", "mixed", "h_sum", "h_y", "h_done", "pads", "firsts", "acc", "du"] +
    ["mm", "gu", "fold", "folded", "down", "mean", "stat", "nat", "route", "cwt", "cwb", "qk", "en", "en_t", "score",
     "att_t", "wt_t",
     "sq", "ln", "rstd", "th", "rexp", "qk_sb", "en_exp", "seg_exp", "att_sb", "fexp", "xs",
     "sum", "x1", "xn", "sg", "su", "hid", "v", "vpart", "cen", "x", "gz", "g1", "g2", "rt", "cw", "cwr", "en_max",
     "en_rec", "sg_s", "sg_p", "ft", "wm", "wt", "bn", "y", "resid", "att"])


def build(nc, pack, w_in, w_x, w_bc, w_dt, x_in_w, x_proj_w, x_dt_w, w_out, w_fgu, w_fdn, w_egu, w_edn,
          w_qk, ebias, w_qo, pm, xT, ctxT, out):
    f32, f32r, u32 = mybir.dt.float32, mybir.dt.float32r, mybir.dt.uint32
    ALU, ACT, AX = mybir.AluOpType, mybir.ActivationFunctionType, mybir.AxisListType
    with ExitStack() as ctx:
        def sb(name, shape, dt=f32):
            return ctx.enter_context(nc.sbuf_tensor(name, shape, dt))

        s = {n: ctx.enter_context(nc.semaphore(n)) for n in SIGNALS}
        every = range(min(x.num for x in s.values()), max(x.num for x in s.values()) + 1)
        ps = ctx.enter_context(nc.psum_tensor("ps", [P, 8, 512], f32))

        pk = sb("pk", [P, PACK])
        wseg = sb("wseg", [P, KC, P])
        pseg = sb("pseg", [P, HID])
        eb = sb("eb", [EXR, HID])
        sel = sb("sel", [2 * BC, BC], f32r)
        selE = sb("selE", [64, ROUTED * 4], f32r)
        selM = sb("selM", [64, len(MIXED), P], f32r)
        cwr = sb("cwr", [64, TOK], f32r)
        ring = sb("ring", [P, NSLOT, SLOT])
        ucv = sb("ucv", [P, UC, TOK])
        yg = sb("yg", [P, UC, TOK])
        yb = sb("yb", [P, 4, TOK])
        dl = sb("dl", [P, 4, TOK])
        du = sb("du", [P, 4, TOK])
        ya = sb("ya", [P, 4, TOK])
        da = sb("da", [P, 2, 4 * TOK])
        hb = sb("hb", [P, 2, 4 * TOK])
        hr_ = sb("hr", [P, TOK])
        tn = sb("tn", [P, TOK])
        bcf = sb("bcf", [BC, TOK])
        bcr = sb("bcr", [2 * BC, TOK], f32r)
        bcx = sb("bcx", [2 * BC, TOK], f32r)
        X = sb("X", [P, KC, TOK])
        V = sb("V", [P, KC, TOK])
        T1 = sb("T1", [P, KC, TOK])
        T2 = sb("T2", [P, KC, TOK])
        R = sb("R", [P, TOK])
        hid = sb("hid", [P, HIDMAX, TOK])
        sm = sb("sm", [P, 256])

        def c(name, i=0, n=1, parts=P):
            return pk[0:parts, COL[name] + i:COL[name] + i + n]

        def dav(i):
            return da[:, i, :].rearrange("p (c t) -> p c t", t=TOK)

        def hbv(i):
            return hb[:, i, :].rearrange("p (c t) -> p c t", t=TOK)

        ident, ones = c("ident", 0, P), c("ones", 0, P)
        hr = hr_[:, :]
        tnx = bcf[0:RANKB, :]
        hx = dav(0)
        up = hb[:, 1, 0:2 * (TOK + 3)].rearrange("p (i t) -> p i t", t=TOK + 3)
        cv = dav(1)[:, 0:2, :]
        ht = dav(1)[:, 2:4, :]
        cx = dav(0)[:, 0:CC, :]
        att = T2
        qT, kT = hid[:, 4, :], hid[:, 5, :]
        tcx = hid[:, 8:8 + CC, :]
        S = hid[:, 8, :]
        aT = hid[:, 9, :]
        th = T1[:, 0:2, :]

        def erow(n):
            return hid[:, 6 + n % 2, :]

        at = [0]

        def small(n):
            at[0] += n
            return sm[:, at[0] - n:at[0]]

        rm, re, rp, rf, ra, rb, rc = (small(TT * EXP).rearrange("p (t e) -> p t e", e=EXP) for _ in range(7))
        rs = small(TT)
        rw = small(TT * 2).rearrange("p (t e) -> p t e", e=2)
        r4, nmax, esum = small(TT), small(TT), small(TT)
        ri = sb("ri", [P, TT, EXP], u32)
        smx = sb("smx", [P, P])
        fl = hid[:, 6, 0:TT * EXR].rearrange("p (t e) -> p t e", e=EXR)
        fr = hid[:, 6, TT * EXR:2 * TT * EXR].rearrange("p (t e) -> p t e", e=EXR)
        fw = hid[:, 7, 0:TT * EXR].rearrange("p (t e) -> p t e", e=EXR)
        wT = hid[0:EXR, 10, :]
        bn = sb("bn", [P, TT, 6])
        mv = sb("mv", [P, TT, 2])
        Aneg = c("A_logA", 0, 12 * NST).rearrange("p (c n) -> p c n", n=NST)

        def wide(ap, n):
            return ap.unsqueeze(1).to_broadcast([ap.shape[0], n, ap.shape[-1]])

        BDk = hid[:, 0, 0:128].rearrange("p (c j) -> p c j", j=8)
        BDv = hid[:, 2:6, :].rearrange("p a t -> p (a t)").rearrange("p (c m) -> p c m", m=P)
        BDn = hid[:, 1, 0:128].rearrange("p (c j) -> p c j", j=8)
        with nc.Block() as block:
            @block.sync
            def _(sp):
                sp.dma_start(pk[:, :], pack).then_inc(s["x_in"], 16)
                sp.dma_start(eb[:, :], ebias).then_inc(s["x_in"], 16)

            @block.gpsimd
            def _(pool):
                pool.memset(BDk[:, :, :], 0.0).then_inc(s["pads"], 1)
                pool.memset(BDn[:, :, :], 0.0).then_inc(s["pads"], 1)
                pool.memset(BDv[:, :, :], 0.0).then_inc(s["pads"], 1)
                pool.memset(cwr[:, :].bitcast(u32), 0).then_inc(s["pads"], 1)

            @block.scalar
            def _(act):
                act.wait_ge(s["pads"], 4)
                for h2 in range(2):
                    for kv, dst in ((0, BDk), (1, BDn)):
                        act.dma_start(dst[64 * h2:64 * h2 + 64, :, SEG * h2:SEG * h2 + SEG],
                                      pm[kv, 64 * h2:64 * h2 + 64, :, 0:SEG]).then_inc(s["ctx_in"], 16)
                act.wait_ge(s["x_in"], 32)
                act.activation(Aneg[:, 0:UC, :].rearrange("p c n -> p (c n)"), c("A_logA", 0, UC * NST),
                               ACT.Exp).then_inc(s["sq"], 1)
                act.activation(Aneg[:, UC:, :].rearrange("p c n -> p (c n)"), c("A_logB", 0, 4 * NST),
                               ACT.Exp).then_inc(s["sq"], 1)

            @block.vector
            def _(dve):
                dve.wait_ge(s["x_in"], 32)
                dve.wait_ge(s["sq"], 2)
                dve.tensor_scalar(Aneg[:, :, :], Aneg[:, :, :], -1.0, None, ALU.mult)
                for name, n in (("conv_bA", UC), ("conv_wA", UC * TAPS), ("conv_bB", 4), ("conv_wB", 4 * TAPS)):
                    dve.tensor_scalar(c(name, 0, n), c(name, 0, n), 0.5, None, ALU.mult)
                dve.tensor_copy(sel[0:BC, :], c("ident", 0, BC, BC))
                dve.tensor_copy(sel[BC:2 * BC, :], c("ident", 0, BC, BC))
                dve.tensor_copy(selE[:, :], c("group", 0, ROUTED * 4, 64))
                for i, k in enumerate(MIXED):
                    dve.tensor_copy(selM[:, i, :].rearrange("p (a b) -> p a b", b=32),
                                    c("group", 4 * k, 4, 64).unsqueeze(2).to_broadcast([64, 4, 32]))
                dve.wait_ge(s["ctx_in"], 64)
                dve.wait_ge(s["pads"], 4)
                for k in range(FOLDS):
                    dve.tensor_copy(BDv[:, k, 8 * k:8 * k + 8], BDn[:, k, :])
        nc.all_engine_barrier(sems_to_clear=every)

        def loads(order, tail):
            fold, down, n = 0, 0, []
            for t, i in order:
                if t == "h_proj" and i % 2 == 0:
                    n.append((w_in[i // 2], "h_mm", 4 * tail + i + 2))
                elif t == "h_bc":
                    n.append((w_x, "h_tr", tail + 1))
                    n.append((w_bc, "h_tr", tail + 2))
                elif t == "h_dt":
                    a = i - tail
                    n.append((w_dt[:, 512 * a:512 * a + 512] if a >= 0 else x_dt_w, "h_dtm", 4 * i + 4))
                elif t == "h_ctx" and i == 0:
                    n.append((x_in_w, "h_mm", 4))
                elif t == "h_ctxbc":
                    n.append((x_proj_w, "h_tr", 1))
                elif t == "seg_fold":
                    n.append((w_qo[i], "folded", i + 1))
                elif t == "h_mix":
                    n.append((w_out[i], "mm", i + 1))
                elif t == "ffn_mm":
                    n.append((w_fgu[i], "gu", i + 1))
                elif t == "exp_mm":
                    n.append((w_egu[i], "gu", FA + i + 1))
                elif t in ("ffn_down", "exp_down"):
                    lo, hi = span(t, i)
                    w = w_fdn if t == "ffn_down" else w_edn
                    m = min(2, hi - i)
                    src = w[i:i + m].rearrange("c p m -> p c m")
                    if i + m < hi:
                        fold += 1
                        n.append((src, "fold", fold))
                    else:
                        down += KC
                        n.append((src, "down", down))
                elif t == "att_qk":
                    n.append((w_qk, "qk", 2))
            return n

        def run(bt, scan, bp):
            proj, tail = bp is not None, int(bt is not None)
            order = schedule(tail, scan, proj)
            units = tail + 2 * scan

            with nc.Block(no_gpsimd_drain=True) as block:
                @block.sync
                def _(sp):
                    if tail:
                        sp.dma_start(cx, ctxT[bass.ds(bt, 1)].rearrange("b p k t -> (b p) k t")).then_inc(s["ctx_in"], 16)
                    todo = loads(order, tail)
                    for k, (src, name, value) in enumerate(todo):
                        if k >= NSLOT:
                            sp.wait_ge(s[todo[k - NSLOT][1]], todo[k - NSLOT][2])
                        shape = src.shape
                        if len(shape) == 3:
                            dst = ring[:, k % NSLOT, 0:shape[1] * shape[2]].rearrange("p (a m) -> p a m", m=shape[2])
                        else:
                            dst = ring[0:shape[0], k % NSLOT, 0:shape[1]]
                        sp.dma_start(dst, src).then_inc(s[f"slot{k % NSLOT}"], 16)
                    if tail:
                        for t in range(TT):
                            sp.wait_ge(s["y"], t + 1)
                            sp.dma_start(out[bass.ds(bt, 1), t * P:(t + 1) * P, :].rearrange("b p h -> (b p) h"),
                                         V[:, t, :]).then_inc(s["out_done"], 16)
                        sp.wait_ge(s["out_done"], 16 * TT)

                @block.tensor
                def _(pe):
                    used = [0]
                    lnk = [0]
                    folds = [0]

                    def slot():
                        k = used[0]
                        used[0] += 1
                        pe.wait_ge(s[f"slot{k % NSLOT}"], 16 * (k // NSLOT + 1))
                        return ring[:, k % NSLOT, :]

                    cur = {}

                    def turn(n):
                        pe.wait_ge(s["en_exp"], n + 1)
                        if n:
                            pe.wait_ge(s["att"], n)
                        for k in range(KC):
                            i = pe.transpose(ps[:, 2, k * P:(k + 1) * P], erow(n)[:, k * P:(k + 1) * P], ident)
                        i.then_inc(s["en_t"], 1)

                    def weights_of(n):
                        r = n - SHARED
                        if r >= 0:
                            if r == 0:
                                pe.wait_ge(s["cwr"], 2)
                            else:
                                pe.wait_ge(s["hid"], FA + n)
                            w = (selM[:, MIXED.index(r), :] if r in MIXED
                                 else selE[:, 4 * r:4 * r + 1].to_broadcast([64, P]))
                            pe.matmul(ps[:, 4, :], w, cwr[:, :], start=True, stop=True).then_inc(s["cwb"], 1)

                    def down(first, lo, hi, done):
                        w = slot()
                        for k in range(first, min(first + 2, hi)):
                            base = (k - lo) % 2 * HID
                            for m in range(KC):
                                if m == 0:
                                    pe.wait_ge(s["hid"], done + hi - lo if k == lo else done + k - lo + 1)
                                i = pe.matmul(ps[:, m, :], w[:, base + m * P:base + (m + 1) * P], hid[:, k - lo, :],
                                              start=(k == lo), stop=(k == hi - 1))
                                if k == hi - 1:
                                    i.then_inc(s["down"], 1)
                            if (k - lo) % 2 == 1 and k < hi - 1:
                                i.then_inc(s["fold"], 1)

                    for t, n in order:
                        if t == "h_norm":
                            if scan:
                                pe.wait_ge(s["mixed"], KC)
                            pe.wait_ge(s["h_sum"], KC - 1)
                            pe.matmul(ps[:, 5, :], ones, hbv(0)[:, 0, :], start=True, stop=True).then_inc(s["h_stat"], 1)
                        elif t == "h_proj":
                            if n % 2 == 0:
                                cur["h"] = slot()
                            if n == 0:
                                pe.wait_ge(s["h_ln"], 1)
                            elif n >= 3:
                                if n - 3 < UC:
                                    pe.wait_ge(s["h_up"], 4 * tail + n - 2)
                                else:
                                    pe.wait_ge(s["h_gz"], n - 2 - UC)
                            for k in range(KC):
                                if n == 0:
                                    pe.wait_ge(s["h_xn"], k + 1)
                                o = (n % 2) * KC * P + k * P
                                i = pe.matmul(ps[:, 5 + n % 3, :], cur["h"][:, o:o + P], hx[:, k, :],
                                              start=(k == 0), stop=(k == KC - 1))
                            i.then_inc(s["h_mm"], 1)
                        elif t == "h_bc":
                            w = slot()
                            pe.wait_ge(s["h_gz"], UC)
                            for k in range(UC):
                                pe.wait_ge(s["h_u"], 4 * tail + k + 1)
                                i = pe.matmul(ps[:, 5, :], w[:, k * P:(k + 1) * P], ucv[:, k, :],
                                              start=(k == 0), stop=(k == UC - 1))
                            i.then_inc(s["h_tr"], 1)
                            w = slot()
                            for k in range(UC):
                                i = pe.matmul(ps[0:BC, 6, :], w[:, k * BC:(k + 1) * BC], ucv[:, k, :],
                                              start=(k == 0), stop=(k == UC - 1))
                            i.then_inc(s["h_tr"], 1)
                        elif t == "h_bn":
                            pe.wait_ge(s["h_bsq"], 1)
                            pe.matmul(ps[:, 7, :], ones, tn[:, :], start=True, stop=True).then_inc(s["h_tstat"], 1)
                            pe.wait_ge(s["h_tn"], tail + 1)
                            pe.wait_ge(s["h_bsq"], 2)
                            pe.matmul(ps[0:BC, 5, :], c("blk", 0, BC, BC), bcf[:, :], start=True, stop=True)\
                                .then_inc(s["h_bstat"], 1)
                        elif t == "h_ctx":
                            if n == 0:
                                cur["h"] = slot()
                                pe.wait_ge(s["ctx_in"], 16)
                            if n == 3:
                                pe.wait_ge(s["h_up"], 1)
                            for k in range(CC):
                                o = (n * CC + k) * P
                                i = pe.matmul(ps[:, 5 + n % 3, :], cur["h"][:, o:o + P], cx[:, k, :],
                                              start=(k == 0), stop=(k == CC - 1))
                            i.then_inc(s["h_mm"], 1)
                        elif t == "h_ctxbc":
                            w = slot()
                            pe.wait_ge(s["h_up"], 4)
                            for k in range(4):
                                pe.wait_ge(s["h_u"], k + 1)
                                i = pe.matmul(ps[0:ROWSB, 5, :], w[:, k * ROWSB:(k + 1) * ROWSB], yb[:, k, :],
                                              start=(k == 0), stop=(k == 3))
                            i.then_inc(s["h_tr"], 1)
                        elif t == "h_dt":
                            w = slot()
                            a = n - tail
                            rows = P if a >= 0 else RANKB
                            low = tn if a >= 0 else tnx
                            if n:
                                pe.wait_ge(s["hc"], NST * n)
                            elif tail:
                                pe.wait_ge(s["h_tn"], 1)
                                pe.wait_ge(s["h_bc"], 2)
                            for k in range(4):
                                if k == 3:
                                    pe.wait_ge(s["dt_abs"], 4 * n + 1)
                                pe.matmul(ps[:, 5 + k % 3, :], w[0:rows, k * P:(k + 1) * P], low[0:rows, :],
                                          start=True, stop=True).then_inc(s["h_dtm"], 1)
                        elif t == "h_scan":
                            u, m = divmod(n, NST)
                            bc = bcr if u >= tail else bcx
                            if m == 0:
                                pe.wait_ge(s["dt_abs"], 4 * u + 4)
                                if u < tail:
                                    pe.wait_ge(s["h_bc"], 2)
                                pe.matmul(ps[:, 5 + n % 2, :], sel[:, 0:1].to_broadcast([2 * BC, P]), bc[:, :],
                                          start=True, stop=True).then_inc(s["b_row"], 1)
                            if m < NST - 1:
                                if m:
                                    pe.wait_ge(s["dbu"], n)
                                pe.matmul(ps[:, 5 + (n + 1) % 2, :], sel[:, m + 1:m + 2].to_broadcast([2 * BC, P]),
                                          bc[:, :], start=True, stop=True).then_inc(s["b_row"], 1)
                            if m:
                                pe.wait_ge(s["hc"], n)
                            pe.matmul(ps[:, 7, :], sel[:, NST + m:NST + m + 1].to_broadcast([2 * BC, P]),
                                      bc[:, :], start=True, stop=True).then_inc(s["c_row"], 1)
                        elif t == "seg_fold":
                            w = slot()
                            for m in range(KC):
                                pe.matmul(ps[:, m, 8 * n:8 * n + 8], w[:, m * P:(m + 1) * P],
                                          BDk[:, n, :], start=True, stop=True)
                            pe.matmul(ps[:, 4, :], BDv[:, n, :], w[:, HID:], start=(n == 0), stop=(n == FOLDS - 1))\
                                .then_inc(s["folded"], 1)
                        elif t == "h_mix":
                            w = slot()
                            if n == 0:
                                pe.wait_ge(s["h_done"], units)
                            elif n == 3:
                                pe.wait_ge(s["mixed"], 1)
                            for k in range(UC):
                                i = pe.matmul(ps[:, 5 + n % 3, :], w[:, k * P:(k + 1) * P], yg[:, k, :],
                                              start=(k == 0), stop=(k == UC - 1))
                            i.then_inc(s["mm"], 1)
                        elif t == "t_norm":
                            pe.wait_ge(s["sum"], KC - 1)
                            pe.matmul(ps[:, 0, :], ones, T1[:, 0, :], start=True, stop=True).then_inc(s["stat"], 1)
                        elif t in ("ffn_mm", "exp_mm"):
                            w = slot()
                            f = n if t == "ffn_mm" else FA + n
                            src, g = (T2, 0) if t == "ffn_mm" else (X, 0)
                            b0 = 2 * (n % 2)
                            if t == "ffn_mm" and n < 2:
                                if n == 0:
                                    pe.wait_ge(s["ln"], 1)
                            elif t == "exp_mm" and any(n in (lo, lo + 1) for lo, _ in PASSES):
                                if n == 0:
                                    pe.wait_ge(s["x"], 8)
                                elif n == 1:
                                    pe.wait_ge(s["att"], TT)
                                else:
                                    p = [lo for lo, _ in PASSES].index(n - n % 2)
                                    pe.wait_ge(s["vpart"], 4 * p - 2 + 2 * (n % 2))
                            else:
                                pe.wait_ge(s["hid"], f - 1)
                            if t == "exp_mm" and n > span(t, n)[0]:
                                weights_of(n - 1)
                            for g in range(2):
                                for k in range(KC):
                                    if t == "ffn_mm" and n == 0 and g == 0:
                                        pe.wait_ge(s["xn"], k + 1)
                                    o = (g * KC + k) * P
                                    i = pe.matmul(ps[:, b0 + g, :], w[:, o:o + P], src[:, k, :],
                                                  start=(k == 0), stop=(k == KC - 1))
                            i.then_inc(s["gu"], 1)
                        elif t == "exp_ev":
                            if n + 1 == span(t, n)[1]:
                                weights_of(n)
                        elif t == "ffn_down":
                            down(n, 0, FA, 0)
                        elif t == "exp_down":
                            lo, hi = span(t, n)
                            down(n, lo, hi, FA + lo)
                        elif t in ("ln_a", "ln_b") and n >= POOLED:
                            done = (KC - 1) * (2 + 2 * (n - POOLED) + (t == "ln_b"))
                            pe.wait_ge(s["sum"], done)
                            if t == "ln_a":
                                pe.matmul(ps[:, 0, :], ones, R[:, :], start=True, stop=True).then_inc(s["mean"], 1)
                            else:
                                pe.matmul(ps[:, 1, :], ones, T1[:, 0, :], start=True, stop=True).then_inc(s["stat"], 1)
                        elif t == "ln_a":
                            for k in range(KC):
                                pe.wait_ge(s["v"], 4 * n + (4 if k == 0 else k + 1))
                                i = pe.matmul(ps[:, 0, :], ones, V[:, k, :], start=(k == 0), stop=(k == KC - 1))
                            i.then_inc(s["mean"], 1)
                        elif t == "ln_b":
                            for k in range(KC):
                                pe.wait_ge(s["sq"], 4 + 4 * n + k + 1 + (4 if n > 2 else 0))
                                i = pe.matmul(ps[:, 1, :], ones, T1[:, k, :], start=(k == 0), stop=(k == KC - 1))
                            i.then_inc(s["stat"], 1)
                        elif t == "gate":
                            pe.wait_ge(s["x"], 4)
                            for e in range(TT):
                                for k in range(KC):
                                    i = pe.transpose(ps[:, e, k * P:(k + 1) * P], X[:, k, e * P:(e + 1) * P], ident)
                                i.then_inc(s["nat"], 1)
                        elif t == "route_a":
                            pe.wait_ge(s["x"], 8)
                            pe.wait_ge(s["en_exp"], TT)
                            for e in range(TT):
                                for k in range(KC):
                                    i = pe.matmul(ps[:, 4, e * EXP:(e + 1) * EXP], X[:, k, e * P:(e + 1) * P],
                                                  c("gate", k * EXP, EXP), start=(k == 0), stop=(k == KC - 1))
                            i.then_inc(s["route"], 1)
                        elif t == "route_c":
                            pe.wait_ge(s["cw"], 1)
                            for e in range(TT):
                                i = pe.transpose(ps[0:EXP, 4, e * P:(e + 1) * P], rc[:, e, :], ident)
                            i.then_inc(s["cwt"], 1)
                        elif t == "att_qk":
                            w = slot()
                            pe.wait_ge(s["tctx_in"], 16)
                            for g in range(2):
                                if g:
                                    pe.wait_ge(s["qk_sb"], 1)
                                for k in range(CC):
                                    o = (g * CC + k) * P
                                    i = pe.matmul(ps[:, 4, :], w[:, o:o + P], tcx[:, k, :],
                                                  start=(k == 0), stop=(k == CC - 1))
                                i.then_inc(s["qk"], 1)
                            pe.wait_ge(s["qk_sb"], 2)
                        elif t == "att_row":
                            if n == 0:
                                pe.wait_ge(s["g1"], TT)
                            if n >= 2:
                                pe.wait_ge(s["en_exp"], n - 1)
                            pe.matmul(ps[:, 3 + n % 2, :], qT[:, n * P:(n + 1) * P], kT, start=True, stop=True)\
                                .then_inc(s["en"], 1)
                            if n:
                                turn(n - 1)
                            if n == TT - 1:
                                turn(n)
                        elif t == "seg_a":
                            pe.wait_ge(s["x"], 12)
                            for e in range(TT):
                                for k in range(KC):
                                    i = pe.matmul(ps[:, 2, e * P:(e + 1) * P], X[:, k, e * P:(e + 1) * P],
                                                  wseg[:, k, :], start=(k == 0), stop=(k == KC - 1))
                            i.then_inc(s["score"], 1)
                            pe.wait_ge(s["sq"], 4 + 12 + 4)
                            for e in range(TT):
                                for k in range(KC):
                                    i = pe.matmul(ps[:, 0, e:e + 1], T1[:, k, e * P:(e + 1) * P],
                                                  ones[:, 0:1], start=(k == 0), stop=(k == KC - 1))
                            i.then_inc(s["stat"], 1)
                        elif t == "seg_b":
                            pe.wait_ge(s["sg_p"], 1)
                            for e in range(TT):
                                i = pe.transpose(ps[:, 3, e * P:(e + 1) * P], S[:, e * P:(e + 1) * P], ident)
                            i.then_inc(s["att_t"], 1)
                            pe.wait_ge(s["att_sb"], 1)
                            for m in range(KC):
                                pe.matmul(ps[:, m, :], pseg[:, m * P:(m + 1) * P], aT, start=True, stop=True)\
                                    .then_inc(s["down"], 1)
                        elif t == "xmix":
                            pe.wait_ge(s["x"], 16)
                            pe.wait_ge(s["att"], TT)
                            for m in range(KC):
                                for k in range(KC):
                                    i = pe.matmul(ps[:, m, :], att[:, k, m * P:(m + 1) * P], X[:, k, :],
                                                  start=(k == 0), stop=(k == KC - 1))
                                i.then_inc(s["down"], 1)
                        elif t == "bias_a":
                            pe.wait_ge(s["x"], 20)
                            for e in range(TT):
                                for k in range(KC):
                                    i = pe.matmul(ps[:, 0, e * EXR:(e + 1) * EXR], X[:, k, e * P:(e + 1) * P],
                                                  c("router", k * EXR, EXR), start=(k == 0), stop=(k == KC - 1))
                            i.then_inc(s["route"], 1)
                            for e in range(TT):
                                for k in range(KC):
                                    i = pe.transpose(ps[:, 1 + e, k * P:(k + 1) * P], X[:, k, e * P:(e + 1) * P], ident)
                                i.then_inc(s["nat"], 1)
                        elif t == "bias_b":
                            pe.wait_ge(s["wm"], 1)
                            for e in range(TT):
                                i = pe.transpose(ps[0:EXR, 0, e * P:(e + 1) * P], fw[:, e, :], ident)
                            i.then_inc(s["wt_t"], 1)
                        elif t == "bias_c":
                            pe.wait_ge(s["wt"], 1)
                            for e in range(TT):
                                pe.wait_ge(s["xs"], e + 1)
                                pe.matmul(ps[:, 1 + e, :], wT[:, e * P:(e + 1) * P], eb[:, :], start=True, stop=True)\
                                    .then_inc(s["down"], 1)

                @block.scalar
                def _(act):
                    cnt = {"ln": 0, "h_ln": 0}

                    def rstd(dst, src, key, eps, parts=P, scale=1.0):
                        pre = "h_" if key == "h" else ""
                        n = cnt[pre + "ln"] = cnt[pre + "ln"] + 1
                        act.preload_act_table_set("natural_log_exp_and_others")
                        act.activation(dst, src, ACT.Ln, bias=c("eps", eps, 1, parts), scale=scale).then_inc(s[pre + "ln"], 1)
                        act.wait_ge(s[pre + "ln"], n)
                        act.activation(dst, dst, ACT.Exp, scale=-0.5).then_inc(s[pre + "rstd"], 1)

                    def fetch():
                        if units:
                            act.wait_ge(s["h_done"], units)
                        act.dma_start(hx, xT[bass.ds(bp, 1)].rearrange("b p k t -> (b p) k t")).then_inc(s["hx_in"], 16)

                    if tail:
                        act.dma_start(X[:, :, :], xT[bass.ds(bt, 1)].rearrange("b p k t -> (b p) k t")).then_inc(s["x_in"], 16)
                    for t, n in order:
                        if t == "h_norm":
                            if not scan:
                                fetch()
                            act.wait_ge(s["hx_in"], 16)
                            for k in range(KC):
                                act.activation(hbv(0)[:, k, :], hx[:, k, :], ACT.Square).then_inc(s["h_sq"], 1)
                            act.wait_ge(s["h_stat"], 1)
                            rstd(hr, ps[:, 5, :], "h", 0)
                        elif t == "h_proj" and n < UC or t == "h_ctx":
                            k = n + 4 * tail if t == "h_proj" else n
                            act.wait_ge(s["h_mm"], k + 1)
                            act.wait_ge(s["pads"], 1 + tail if t == "h_proj" else 1)
                            if n >= 2:
                                act.wait_ge(s["h_conv"], k - 1)
                            act.activation(up[:, n % 2, 3:], ps[:, 5 + n % 3, :], ACT.Copy).then_inc(s["h_up"], 1)
                            act.wait_ge(s["h_conv"], k + 1)
                            if n >= 2:
                                act.wait_ge(s["h_u"], k - 1)
                            act.activation(ht[:, n % 2, :], cv[:, n % 2, :], ACT.Tanh).then_inc(s["h_th"], 1)
                        elif t == "h_proj":
                            g = n - UC
                            act.wait_ge(s["h_mm"], 4 * tail + n + 1)
                            if g < 2:
                                act.wait_ge(s["h_u"], 4 * tail + UC - 1 + g)
                            else:
                                act.wait_ge(s["h_gz"], g - 1)
                            act.activation(ht[:, n % 2, :], ps[:, 5 + n % 3, :], ACT.Tanh, scale=0.5).then_inc(s["h_th"], 1)
                        elif t == "h_bc":
                            act.wait_ge(s["h_tr"], tail + 1)
                            act.activation(tn[:, :], ps[:, 5, :], ACT.Square).then_inc(s["h_bsq"], 1)
                            act.wait_ge(s["h_tr"], tail + 2)
                            act.activation(bcf[:, :], ps[0:BC, 6, :], ACT.Square).then_inc(s["h_bsq"], 1)
                        elif t == "h_bn":
                            act.wait_ge(s["h_tstat"], 1)
                            rstd(hr, ps[:, 7, :], "h", 0, scale=float(HID) / RANK)
                            act.wait_ge(s["h_bstat"], 1)
                            act.wait_ge(s["h_tn"], tail + 1)
                            rstd(hr[0:BC], ps[0:BC, 5, :], "h", 0, parts=BC)
                        elif t == "h_mix":
                            if n == 0 and proj:
                                fetch()
                            act.wait_ge(s["mm"], n + 1)
                            act.activation(du[:, n, :], ps[:, 5 + n % 3, :], ACT.Copy).then_inc(s["mixed"], 1)
                        elif t == "h_dt":
                            act.preload_act_table_set("natural_log_exp_and_others")
                            if n:
                                act.wait_ge(s["h_done"], n)
                            a = n - tail
                            for k in range(4):
                                b = c("dt_bA", 4 * a + k) if a >= 0 else c("dt_bB", k)
                                act.wait_ge(s["h_dtm"], 4 * n + k + 1)
                                act.activation(dl[:, k, :], ps[:, 5 + k % 3, :], ACT.Relu, bias=b)
                                act.activation(hbv(0)[:, k, :], ps[:, 5 + k % 3, :], ACT.Abs, bias=b).then_inc(s["dt_abs"], 1)
                            act.wait_ge(s["dt_abs"], 4 * n + 4)
                            act.activation(hb[:, 0, :], hb[:, 0, :], ACT.Exp, scale=-1.0).then_inc(s["dt_exp"], 1)
                        elif t == "h_dt_b":
                            act.wait_ge(s["dt_one"], n + 1)
                            act.activation(da[:, 0, :], hb[:, 1, :], ACT.Ln).then_inc(s["dt_log"], 1)
                        elif t == "h_scan":
                            u, m = divmod(n, NST)
                            if m == 0:
                                act.wait_ge(s["delta"], u + 1)
                                act.wait_ge(s["firsts"], u + 1)
                            if m >= 2:
                                act.wait_ge(s["scan"], n - 1)
                            for k in range(4):
                                i = act.activation(dav(n % 2)[:, k, 1:], dl[:, k, 1:], ACT.Exp,
                                                   scale=Aneg[:, (4 * (u - tail) if u >= tail else UC) + k, m:m + 1])
                            i.then_inc(s["da"], 1)
                        elif t == "t_norm":
                            for k in range(KC):
                                act.wait_ge(s["x1"], k + 1)
                                act.activation(T1[:, k, :], V[:, k, :], ACT.Square).then_inc(s["sq"], 1)
                            act.wait_ge(s["stat"], 1)
                            rstd(R[:, :], ps[:, 0, :], "t", 0)
                        elif t in ("ffn_ev", "exp_ev"):
                            f = n if t == "ffn_ev" else FA + n
                            act.wait_ge(s["gu"], f + 1)
                            if f >= 2:
                                act.wait_ge(s["hid"], f - 1)
                            act.activation(th[:, f % 2, :], ps[:, 2 * (n % 2), :], ACT.Tanh, scale=0.5)\
                                .then_inc(s["th"], 1)
                        elif t == "ln_a":
                            for k in range(KC):
                                act.wait_ge(s["cen"], 4 * n + k + 1)
                                act.activation(T1[:, k, :], V[:, k, :], ACT.Square).then_inc(s["sq"], 1)
                        elif t == "ln_b":
                            act.wait_ge(s["stat"], n + 2 + (1 if n > 2 else 0))
                            rstd(R[:, :], ps[:, 1, :], "t", 1)
                        elif t == "gate":
                            for e in range(TT):
                                act.wait_ge(s["nat"], e + 1)
                                act.activation(T1[:, e, :], ps[:, e, :], ACT.Tanh, scale=0.5).then_inc(s["gz"], 1)
                        elif t == "route_a":
                            act.wait_ge(s["rt"], 2)
                            act.activation(re[:, :, :], re[:, :, :], ACT.Exp).then_inc(s["rexp"], 1)
                        elif t == "att_qk":
                            act.wait_ge(s["down"], 4)
                            act.dma_start(tcx, ctxT[bass.ds(bt, 1)].rearrange("b p k t -> (b p) k t")).then_inc(s["tctx_in"], 16)
                            for g, (dst, b) in enumerate(((qT, "bq"), (kT, "bk"))):
                                act.wait_ge(s["qk"], g + 1)
                                act.activation(dst, ps[:, 4, :], ACT.Identity, bias=c(b)).then_inc(s["qk_sb"], 1)
                        elif t == "att_row":
                            act.wait_ge(s["en_max"], n + 1)
                            if n >= 2:
                                act.wait_ge(s["en_t"], n - 1)
                            act.activation(erow(n), ps[:, 3 + n % 2, :], ACT.Exp, bias=nmax[:, n:n + 1],
                                           accum_out=esum[:, n:n + 1]).then_inc(s["en_exp"], 1)
                            for m in ([n - 1] if n else []) + ([n] if n == TT - 1 else []):
                                act.wait_ge(s["en_t"], m + 1)
                                act.activation(att[:, :, m * P:(m + 1) * P],
                                               ps[:, 2, :].rearrange("p (k m) -> p k m", m=P), ACT.Copy)\
                                    .then_inc(s["att"], 1)
                        elif t == "seg_a":
                            act.wait_ge(s["x"], 12)
                            for k in range(KC):
                                act.activation(T1[:, k, :], X[:, k, :], ACT.Square).then_inc(s["sq"], 1)
                            act.wait_ge(s["stat"], 5)
                            rstd(r4, ps[:, 0, 0:TT], "t", 2)
                        elif t == "seg_b":
                            act.wait_ge(s["sg_s"], 3)
                            act.activation(S, S, ACT.Exp).then_inc(s["seg_exp"], 1)
                            act.wait_ge(s["att_t"], 1)
                            act.activation(aT, ps[:, 3, :], ACT.Copy).then_inc(s["att_sb"], 1)
                        elif t == "bias_a":
                            act.wait_ge(s["ft"], 3)
                            act.activation(fl[:, :, :], fl[:, :, :], ACT.Exp).then_inc(s["fexp"], 1)
                        elif t == "bias_b":
                            act.wait_ge(s["wm"], 2)
                            for e in range(TT):
                                act.wait_ge(s["nat"], TT + e + 1)
                                act.activation(T1[:, e, :], ps[:, 1 + e, :], ACT.Copy, scale=rs[:, e:e + 1])\
                                    .then_inc(s["xs"], 1)
                        elif t == "bias_c":
                            act.wait_ge(s["bn"], 2)
                            rstd(r4, mv[:, :, 1], "t", 1)

                @block.vector
                def _(dve):
                    vt = [0]

                    def center(n):
                        dve.wait_ge(s["mean"], n + 1)
                        for k in range(KC):
                            dve.tensor_tensor(V[:, k, :], V[:, k, :], ps[:, 0, :], ALU.subtract).then_inc(s["cen"], 1)

                    def evac_sum(base, src, last):
                        for m in range(KC):
                            dve.wait_ge(s["down"], base + m + 1)
                            dve.tensor_tensor(V[:, m, :], ps[:, m, :], src[:, m, :], ALU.add)\
                                .then_inc(s["v" if last else "vpart"], 1)

                    S3 = S.rearrange("p (t h j) -> p t h j", h=HEADS, j=SEG)
                    Sj = S.rearrange("p (h j) -> p h j", j=SEG)
                    mb = smx[:, :].unsqueeze(2).to_broadcast([P, P, SEG])
                    steps = {"rt": 0, "ft": 0}

                    def stage(name, i):
                        steps[name] += 1
                        i.then_inc(s[name], 1)
                        dve.wait_ge(s[name], steps[name])

                    def step(i):
                        stage("rt", i)

                    def fstep(i):
                        stage("ft", i)

                    taps = [0]

                    def conv(k, n, w, b):
                        dve.wait_ge(s["h_up"], k + 1)
                        if n >= 2:
                            dve.wait_ge(s["h_u"], k - 1)
                        dve.tensor_scalar(cv[:, n % 2, :], up[:, n % 2, 3:], c(w, n * TAPS + 3), c(b, n),
                                          ALU.mult, ALU.add).then_inc(s["h_tap"], 1)
                        taps[0] += 1
                        for tap in range(3):
                            dve.wait_ge(s["h_tap"], taps[0])
                            i = dve.scalar_tensor_tensor(out=cv[:, n % 2, :], in0=up[:, n % 2, tap:tap + TOK],
                                                         scalar=c(w, n * TAPS + tap), in1=cv[:, n % 2, :],
                                                         op0=ALU.mult, op1=ALU.add)
                            if tap < 2:
                                i.then_inc(s["h_tap"], 1)
                                taps[0] += 1
                            else:
                                i.then_inc(s["h_conv"], 1)

                    def silu(k, n, seen, u):
                        dve.wait_ge(s["h_th"], seen)
                        dve.scalar_tensor_tensor(out=u[:, n, :], in0=ht[:, n % 2, :], scalar=1.0,
                                                 in1=cv[:, n % 2, :], op0=ALU.add, op1=ALU.mult).then_inc(s["h_u"], 1)

                    for t, n in order:
                        if t == "h_norm":
                            dve.wait_ge(s["h_rstd"], 1)
                            for k in range(KC):
                                dve.scalar_tensor_tensor(out=hx[:, k, :], in0=hx[:, k, :], scalar=c("in_ln", k),
                                                         in1=hr, op0=ALU.mult, op1=ALU.mult).then_inc(s["h_xn"], 1)
                        elif t == "h_proj" and n < UC:
                            conv(4 * tail + n, n, "conv_wA", "conv_bA")
                            silu(4 * tail + n, n, 4 * tail + n + 1, ucv)
                        elif t == "h_proj":
                            g = n - UC
                            dve.wait_ge(s["h_th"], 4 * tail + n + 1)
                            if scan and g == 0:
                                dve.wait_ge(s["mm"], 4)
                            dve.scalar_tensor_tensor(out=yg[:, g, :], in0=ht[:, n % 2, :], scalar=1.0,
                                                     in1=ps[:, 5 + n % 3, :], op0=ALU.add, op1=ALU.mult)\
                                .then_inc(s["h_gz"], 1)
                        elif t == "h_bn":
                            dve.wait_ge(s["h_rstd"], 2)
                            dve.scalar_tensor_tensor(out=tn[:, :], in0=ps[:, 5, :], scalar=c("dt_ln"), in1=hr,
                                                     op0=ALU.mult, op1=ALU.mult).then_inc(s["h_tn"], 1)
                            dve.wait_ge(s["h_rstd"], 3)
                            dve.scalar_tensor_tensor(out=bcf[:, :], in0=ps[0:BC, 6, :], scalar=c("bc_ln", 0, 1, BC),
                                                     in1=hr[0:BC], op0=ALU.mult, op1=ALU.mult).then_inc(s["h_bcf"], 1)
                            dve.wait_ge(s["h_bcf"], 1)
                            dve.tensor_copy(bcr[0:BC, :], bcf[:, :]).then_inc(s["h_bc"], 1)
                            dve.wait_ge(s["h_bc"], 2 * tail + 1)
                            dve.tensor_tensor(bcr[BC:2 * BC, :], bcf[:, :], bcr[0:BC, :].bitcast(f32), ALU.subtract)\
                                .then_inc(s["h_bc"], 1)
                        elif t == "h_ctx":
                            conv(n, n, "conv_wB", "conv_bB")
                            silu(n, n, n + 1, yb)
                        elif t == "h_ctxbc":
                            dve.wait_ge(s["h_tr"], 1)
                            dve.tensor_copy(tnx, ps[0:RANKB, 5, :]).then_inc(s["h_tn"], 1)
                            dve.tensor_copy(bcx[0:BC, :], ps[BC:2 * BC, 5, :]).then_inc(s["h_bc"], 1)
                            dve.wait_ge(s["h_bc"], 1)
                            dve.tensor_tensor(bcx[BC:2 * BC, :], ps[BC:2 * BC, 5, :], bcx[0:BC, :].bitcast(f32), ALU.subtract)\
                                .then_inc(s["h_bc"], 1)
                        elif t == "h_dt_b":
                            dve.wait_ge(s["dt_exp"], n + 1)
                            dve.tensor_scalar(hb[:, 1, :], hb[:, 0, :], 1.0, None, ALU.add).then_inc(s["dt_one"], 1)
                        elif t == "h_dt_c":
                            dve.wait_ge(s["dt_log"], n + 1)
                            dve.scalar_tensor_tensor(out=hb[:, 1, :], in0=hb[:, 1, :], scalar=-1.0, in1=hb[:, 0, :],
                                                     op0=ALU.add, op1=ALU.subtract).then_inc(s["dt_res"], 1)
                            dlf = dl[:, :, :].rearrange("p c t -> p (c t)")
                            dve.wait_ge(s["dt_res"], 3 * n + 1)
                            dve.tensor_tensor(hb[:, 1, :], da[:, 0, :], hb[:, 1, :], ALU.subtract).then_inc(s["dt_res"], 1)
                            dve.wait_ge(s["dt_res"], 3 * n + 2)
                            dve.tensor_tensor(dlf, dlf, hb[:, 1, :], ALU.add).then_inc(s["dt_res"], 1)
                            dve.wait_ge(s["dt_res"], 3 * n + 3)
                            a = n - tail
                            uu = ucv[:, 4 * a:4 * a + 4, :] if a >= 0 else yb[:, :, :]
                            dve.tensor_tensor(du[:, :, :], dl[:, :, :], uu, ALU.mult).then_inc(s["delta"], 1)
                        elif t == "h_scan":
                            u, m = divmod(n, NST)
                            dve.wait_ge(s["b_row"], n + 1)
                            dve.wait_ge(s["delta"], u + 1)
                            if m >= 2:
                                dve.wait_ge(s["acc"], n - 1)
                            dve.tensor_tensor(hbv(n % 2), du[:, :, :], wide(ps[:, 5 + n % 2, :], 4), ALU.mult)\
                                .then_inc(s["dbu"], 1)
                            dve.wait_ge(s["da"], n + 1)
                            dve.wait_ge(s["dbu"], n + 1)
                            dve.tensor_tensor_scan(hb[:, n % 2, :], da[:, n % 2, :], hb[:, n % 2, :], 0.0,
                                                   ALU.mult, ALU.add).then_inc(s["scan"], 1)
                            dve.wait_ge(s["c_row"], n + 1)
                            dve.wait_ge(s["scan"], n + 1)
                            dve.tensor_tensor(hbv(n % 2), hbv(n % 2), wide(ps[:, 7, :], 4), ALU.mult)\
                                .then_inc(s["hc"], 1)
                        elif t == "h_fin":
                            dve.wait_ge(s["acc"], NST * (n + 1))
                            a = n - tail
                            for k in range(4):
                                dst = hbv(0)[:, k, :] if a >= 0 else yb[:, k, :]
                                i = dve.scalar_tensor_tensor(out=dst, in0=ucv[:, 4 * a + k, :] if a >= 0 else dst,
                                                             scalar=c("DA", 4 * a + k) if a >= 0 else c("DB", k),
                                                             in1=ya[:, k, :], op0=ALU.mult, op1=ALU.add)
                            if a < 0:
                                i.then_inc(s["h_done"], 1)
                            else:
                                i.then_inc(s["h_y"], 1)
                                dve.wait_ge(s["h_y"], a + 1)
                                dve.scalar_tensor_tensor(out=yg[:, 4 * a:4 * a + 4, :], in0=hbv(0), scalar=0.5,
                                                         in1=yg[:, 4 * a:4 * a + 4, :], op0=ALU.mult, op1=ALU.mult)\
                                    .then_inc(s["h_done"], 1)
                        elif t == "seg_folded":
                            dve.wait_ge(s["folded"], FOLDS)
                            for k in range(KC):
                                dve.tensor_scalar(wseg[:, k, :], ps[:, k, 0:P], c("seg_ln", k), float(DH) ** -0.5,
                                                  ALU.mult, ALU.mult)
                            dve.tensor_copy(pseg[:, :], ps[:, 4, :])
                        elif t == "x1":
                            dve.wait_ge(s["x_in"], 16)
                            for m in range(KC):
                                dve.tensor_tensor(V[:, m, :], du[:, m, :], X[:, m, :], ALU.add).then_inc(s["x1"], 1)
                        elif t == "t_norm":
                            dve.wait_ge(s["rstd"], 1)
                            for k in range(KC):
                                dve.scalar_tensor_tensor(out=T2[:, k, :], in0=V[:, k, :], scalar=c("pre_ln", k),
                                                         in1=R[:, :], op0=ALU.mult, op1=ALU.mult).then_inc(s["xn"], 1)
                        elif t in ("ffn_ev", "exp_ev"):
                            f = n if t == "ffn_ev" else FA + n
                            lo = 0 if t == "ffn_ev" else max(a for a, _ in PASSES if a <= n)
                            b0 = 2 * (n % 2)
                            dve.wait_ge(s["th"], f + 1)
                            dve.scalar_tensor_tensor(out=th[:, f % 2, :], in0=th[:, f % 2, :], scalar=1.0,
                                                     in1=ps[:, b0, :], op0=ALU.add, op1=ALU.mult).then_inc(s["sg"], 1)
                            dve.wait_ge(s["sg"], f + 1)
                            if t == "exp_ev" and n == 0:
                                dve.wait_ge(s["att"], TT)
                            elif t == "exp_ev" and n == lo:
                                dve.wait_ge(s["down"], 4 * (1 + [a for a, _ in PASSES].index(lo)))
                            plain = t == "ffn_ev" or n < SHARED
                            dst = hid[:, n - lo, :]
                            dve.scalar_tensor_tensor(out=dst, in0=th[:, f % 2, :], scalar=0.5, in1=ps[:, b0 + 1, :],
                                                     op0=ALU.mult, op1=ALU.mult)\
                                .then_inc(s["hid" if plain else "su"], 1)
                            if not plain:
                                dve.wait_ge(s["su"], n - SHARED + 1)
                                dve.wait_ge(s["cwb"], n - SHARED + 1)
                                dve.tensor_tensor(dst, dst, ps[:, 4, :], ALU.mult).then_inc(s["hid"], 1)
                        elif t == "ffn_down" and n + 2 >= FA:
                            dve.wait_ge(s["resid"], 1)
                            evac_sum(0, X, True)
                        elif t == "exp_down" and n + 2 >= span(t, n)[1]:
                            p = PASSES.index(span(t, n))
                            if p:
                                dve.wait_ge(s["vpart"], 4 * p)
                            evac_sum(4 * (p + 1), V if p else X, p == len(PASSES) - 1)
                        elif t == "ln_a":
                            center(n)
                        elif t == "ln_b":
                            dve.wait_ge(s["rstd"], n + 2 + (1 if n > 2 else 0))
                            for k in range(KC):
                                dve.tensor_tensor(X[:, k, :], V[:, k, :], R[:, :], ALU.mult).then_inc(s["x"], 1)
                        elif t == "gate":
                            for e in range(TT):
                                dve.wait_ge(s["gz"], e + 1)
                                dve.scalar_tensor_tensor(out=T2[:, e, :], in0=T1[:, e, :], scalar=1.0, in1=ps[:, e, :],
                                                         op0=ALU.add, op1=ALU.mult).then_inc(s["g1"], 1)
                                dve.wait_ge(s["g1"], e + 1)
                                dve.scalar_tensor_tensor(out=T2[:, e, :], in0=T2[:, e, :], scalar=0.5, in1=yb[:, e, :],
                                                         op0=ALU.mult, op1=ALU.mult).then_inc(s["g2"], 1)
                                dve.wait_ge(s["g2"], e + 1)
                                dve.tensor_tensor(V[:, e, :], T2[:, e, :], X[:, e, :], ALU.add).then_inc(s["v"], 1)
                        elif t == "route_a":
                            pr = ps[:, 4, 0:TT * EXP].rearrange("p (t e) -> p t e", e=EXP)
                            dve.wait_ge(s["route"], 1)
                            for e in range(TT):
                                i = dve.max(rm[:, e, :], pr[:, e, :])
                            step(i)
                            step(dve.tensor_tensor(re[:, :, :], pr, rm[:, :, 0:1].to_broadcast([P, TT, EXP]), ALU.subtract))
                        elif t == "route_b":
                            dve.wait_ge(s["rexp"], 1)
                            step(dve.tensor_reduce(rs, re[:, :, :], AX.X, ALU.add))
                            step(dve.reciprocal(rs, rs))
                            step(dve.tensor_tensor(rp[:, :, :], re[:, :, :], rs.unsqueeze(2).to_broadcast([P, TT, EXP]), ALU.mult))
                            for e in range(TT):
                                i = dve.max(rm[:, e, :], rp[:, e, :])
                            step(i)
                            for e in range(TT):
                                i = dve.max_index(ri[:, e, :], rm[:, e, :], rp[:, e, :])
                            step(i)
                            step(dve.tensor_copy(rf[:, :, :], ri[:, :, :]))
                            step(dve.scalar_tensor_tensor(out=rs, in0=rm[:, :, 0], scalar=1e-20, in1=rm[:, :, 1],
                                                          op0=ALU.add, op1=ALU.add))
                            step(dve.reciprocal(rs, rs))
                            step(dve.tensor_tensor(rw[:, :, :], rm[:, :, 0:2], rs.unsqueeze(2).to_broadcast([P, TT, 2]), ALU.mult))
                            for e in range(TT):
                                dve.tensor_scalar(ra[:, e, :], c("iota", 0, EXP), rf[:, e, 0:1], rw[:, e, 0:1],
                                                  ALU.is_equal, ALU.mult)
                                i = dve.tensor_scalar(rb[:, e, :], c("iota", 0, EXP), rf[:, e, 1:2], rw[:, e, 1:2],
                                                      ALU.is_equal, ALU.mult)
                            step(i)
                            dve.tensor_tensor(rc[:, :, :], ra[:, :, :], rb[:, :, :], ALU.add).then_inc(s["cw"], 1)
                        elif t == "route_c":
                            dve.wait_ge(s["cwt"], 1)
                            dve.tensor_copy(cwr[0:EXP, :], ps[0:EXP, 4, :]).then_inc(s["cwr"], 1)
                            dve.wait_ge(s["cwr"], 1)
                            dve.tensor_tensor(cwr[32:32 + EXP, :], ps[0:EXP, 4, :], cwr[0:EXP, :].bitcast(f32),
                                              ALU.subtract).then_inc(s["cwr"], 1)
                        elif t == "att_row":
                            dve.wait_ge(s["en"], n + 1)
                            dve.tensor_reduce(nmax[:, n:n + 1], ps[:, 3 + n % 2, :], AX.X, ALU.max, negate=True)\
                                .then_inc(s["en_max"], 1)
                            dve.wait_ge(s["en_exp"], n + 1)
                            dve.reciprocal(esum[:, n:n + 1], esum[:, n:n + 1]).then_inc(s["en_rec"], 1)
                        elif t == "seg_a":
                            dve.wait_ge(s["score"], 1)
                            dve.wait_ge(s["rstd"], 5)
                            for e in range(TT):
                                i = dve.scalar_tensor_tensor(
                                    out=S3[:, e], in0=ps[:, 2, e * P:(e + 1) * P].rearrange("p (h j) -> p h j", j=SEG),
                                    scalar=r4[:, e:e + 1], in1=wide(c("mask", 0, SEG), HEADS), op0=ALU.mult, op1=ALU.add)
                            i.then_inc(s["sg_s"], 1)
                            dve.wait_ge(s["sg_s"], 1)
                            dve.tensor_reduce(smx[:, :], Sj, AX.X, ALU.max).then_inc(s["sg_s"], 1)
                            dve.wait_ge(s["sg_s"], 2)
                            dve.tensor_tensor(Sj, Sj, mb, ALU.subtract).then_inc(s["sg_s"], 1)
                        elif t == "seg_b":
                            dve.wait_ge(s["seg_exp"], 1)
                            dve.tensor_reduce(smx[:, :], Sj, AX.X, ALU.add).then_inc(s["sg_s"], 1)
                            dve.wait_ge(s["sg_s"], 4)
                            dve.reciprocal(smx[:, :], smx[:, :]).then_inc(s["sg_s"], 1)
                            dve.wait_ge(s["sg_s"], 5)
                            dve.tensor_tensor(Sj, Sj, mb, ALU.mult).then_inc(s["sg_p"], 1)
                        elif t == "seg_c":
                            evac_sum(16, X, True)
                        elif t == "xmix":
                            for m in range(KC):
                                dve.wait_ge(s["down"], 20 + m + 1)
                                dve.wait_ge(s["en_rec"], TT)
                                dve.scalar_tensor_tensor(out=V[:, m, :], in0=ps[:, m, :], scalar=esum[:, m:m + 1],
                                                         in1=X[:, m, :], op0=ALU.mult, op1=ALU.add).then_inc(s["v"], 1)
                        elif t == "bias_a":
                            pf = ps[:, 0, 0:TT * EXR].rearrange("p (t e) -> p t e", e=EXR)
                            dve.wait_ge(s["route"], 2)
                            fstep(dve.tensor_tensor(fl[:, :, :], pf, wide(c("rbias", 0, EXR), TT), ALU.add))
                            for e in range(TT):
                                i = dve.max(rm[:, e, :], fl[:, e, :])
                            fstep(i)
                            fstep(dve.tensor_tensor(fl[:, :, :], fl[:, :, :], rm[:, :, 0:1].to_broadcast([P, TT, EXR]), ALU.subtract))
                        elif t == "bias_b":
                            dve.wait_ge(s["fexp"], 1)
                            fstep(dve.tensor_reduce(rs, fl[:, :, :], AX.X, ALU.add))
                            fstep(dve.reciprocal(rs, rs))
                            fstep(dve.tensor_tensor(fl[:, :, :], fl[:, :, :], rs.unsqueeze(2).to_broadcast([P, TT, EXR]), ALU.mult))
                            for e in range(TT):
                                i = dve.max(rm[:, e, :], fl[:, e, :])
                            fstep(i)
                            for e in range(TT):
                                i = dve.match_replace(fr[:, e, :], rm[:, e, :], fl[:, e, :], 0.0)
                            fstep(i)
                            dve.tensor_tensor(fw[:, :, :], fl[:, :, :], fr[:, :, :], ALU.subtract).then_inc(s["wm"], 1)
                            fstep(dve.tensor_reduce(rs, rm[:, :, :], AX.X, ALU.add))
                            dve.tensor_scalar(rs, rs, 1.0, None, ALU.add).then_inc(s["wm"], 1)
                        elif t == "bias_c":
                            dve.wait_ge(s["wt_t"], 1)
                            dve.tensor_copy(wT, ps[0:EXR, 0, :]).then_inc(s["wt"], 1)
                            for e in range(TT):
                                dve.wait_ge(s["down"], 24 + e + 1)
                                fstep(dve.tensor_tensor(V[:, e, :], ps[:, 1 + e, :], T1[:, e, :], ALU.add))
                                i = dve.bn_stats(bn[:, e, :], V[:, e, :])
                            i.then_inc(s["bn"], 1)
                            dve.wait_ge(s["bn"], 1)
                            for e in range(TT):
                                i = dve.bn_aggr(mv[:, e, :], bn[:, e, :])
                            i.then_inc(s["bn"], 1)
                            dve.wait_ge(s["rstd"], 8)
                            for e in range(TT):
                                dve.tensor_scalar(V[:, e, :], V[:, e, :], mv[:, e, 0:1], r4[:, e:e + 1],
                                                  ALU.subtract, ALU.mult).then_inc(s["y"], 1)

                @block.gpsimd
                def _(pool):
                    sums = {"sum": 0, "h_sum": 0}

                    def add(name, dst, a, b):
                        if sums[name]:
                            pool.wait_ge(s[name], sums[name])
                        sums[name] += 1
                        pool.tensor_tensor(dst, a, b, ALU.add).then_inc(s[name], 1)

                    if tail or not units:
                        pool.memset(up[:, :, 0:3], 0.0).then_inc(s["pads"], 1)
                    for t, n in order:
                        if t == "t_norm":
                            for k in range(1, KC):
                                pool.wait_ge(s["sq"], k + 1)
                                add("sum", T1[:, 0, :], T1[:, 0, :], T1[:, k, :])
                            pool.wait_ge(s["x1"], 4)
                            pool.tensor_tensor(X[:, :, :], X[:, :, :], V[:, :, :], ALU.add).then_inc(s["resid"], 1)
                        elif t == "ln_a" and n >= POOLED:
                            for k in range(1, KC):
                                pool.wait_ge(s["v"], 4 * n + k + 1)
                                add("sum", R[:, :], R[:, :] if k > 1 else V[:, 0, :], V[:, k, :])
                        elif t == "ln_b" and n >= POOLED:
                            for k in range(1, KC):
                                pool.wait_ge(s["sq"], 4 + 4 * n + k + 1 + (4 if n > 2 else 0))
                                add("sum", T1[:, 0, :], T1[:, 0, :], T1[:, k, :])
                        elif t == "h_norm":
                            if units:
                                pool.wait_ge(s["h_done"], units)
                                pool.memset(up[:, :, 0:3], 0.0).then_inc(s["pads"], 1)
                            for k in range(1, KC):
                                pool.wait_ge(s["h_sq"], k + 1)
                                add("h_sum", hbv(0)[:, 0, :], hbv(0)[:, 0, :], hbv(0)[:, k, :])
                        elif t == "h_scan":
                            u, m = divmod(n, NST)
                            if m == 0:
                                pool.wait_ge(s["delta"], u + 1)
                                pool.memset(da[:, :, :].rearrange("p i (c t) -> p (i c) t", t=TOK)[:, :, 0:1], 0.0)\
                                    .then_inc(s["firsts"], 1)
                            pool.wait_ge(s["hc"], n + 1)
                            if m == 0:
                                if u:
                                    pool.wait_ge(s["h_done"], u)
                                pool.tensor_copy(ya[:, :, :], hbv(n % 2)).then_inc(s["acc"], 1)
                            else:
                                pool.wait_ge(s["acc"], n)
                                pool.tensor_tensor(ya[:, :, :], ya[:, :, :], hbv(n % 2), ALU.add).then_inc(s["acc"], 1)
            nc.all_engine_barrier(sems_to_clear=every)

        run(None, False, 0)
        run(None, True, 1)
        with nc.Fori(0, SEQS - 2) as b:
            run(b, True, b + 2)
        run(SEQS - 2, True, None)
        run(SEQS - 1, False, None)


def kernel(**inputs):
    import numpy as np
    import concourse.bacc as _bacc
    from concourse import mybir as _mybir
    from concourse.bass_utils import run_bass_kernel_spmd as _run

    g = {k: np.asarray(v) for k, v in inputs.items()}
    f = np.float32

    def cols(v, n):
        v = v.reshape((n, P) + v.shape[1:])
        return np.moveaxis(v, 0, 1).reshape(P, -1)

    def tiles(w, mc, kc):
        return np.ascontiguousarray(w.reshape(mc, P, kc, P).transpose(0, 3, 2, 1)).reshape(mc, P, kc * P)

    pack = np.zeros((P, PACK), f)

    def put(name, v):
        v = v.reshape(v.shape[0], -1)
        pack[:v.shape[0], COL[name]:COL[name] + v.shape[1]] = v

    A, B, M, D, E, F = "L0_attn_", "L0_xattn_", "L0_ffn_", "L1_attn_", "L1_xattn_", "L1_ffn_"
    put("in_ln", cols(g[A + "input_ln_w"], KC))
    put("pre_ln", cols(g[A + "pre_ff_ln_w"], KC))
    put("conv_bA", cols(g[A + "conv_b"], UC))
    put("conv_wA", cols(g[A + "conv_w"].reshape(DI, TAPS), UC))
    put("dt_bA", cols(g[A + "b_dt"], UC))
    put("DA", cols(g[A + "D_skip"], UC))
    put("A_logA", cols(g[A + "A_log"], UC))
    put("dt_ln", g[A + "dt_ln_w"])
    put("bc_ln", np.concatenate([g[A + "b_ln_w"], g[A + "c_ln_w"]]))
    put("conv_bB", cols(g[B + "conv_b"], 4))
    put("conv_wB", cols(g[B + "conv_w"], 4))
    put("dt_bB", cols(g[B + "dt_proj_b"], 4))
    put("DB", cols(g[B + "D"], 4))
    put("A_logB", cols(g[B + "A_log"], 4))
    put("seg_ln", cols(g[D + "w_norm"], KC))
    put("bq", g[E + "bq"])
    put("bk", g[E + "bk"])
    put("eps", np.broadcast_to(np.array([EPS, EPS_LN, EPS_SEG], f), (P, 3)))
    put("mask", np.where(np.arange(SEG)[None] <= np.arange(P)[:, None] % SEG, 0, NEG).astype(f))
    put("iota", np.broadcast_to(np.arange(EXP, dtype=f), (P, EXP)))
    put("blk", (np.arange(BC)[:, None] // NST == np.arange(BC)[None] // NST).astype(f) / NST)
    rows = np.arange(64)
    put("group", ((rows[:, None] % 32 == np.arange(ROUTED * 4)[None] // (FE // 32)) & (rows[:, None] % 32 < EXP)).astype(f))
    put("ident", np.eye(P, dtype=f))
    put("gate", cols(np.ascontiguousarray(g[M + "gate_weight"].T), KC))
    put("router", cols(np.ascontiguousarray(g[F + "router_weight"].T), KC))
    put("rbias", np.broadcast_to(g[F + "router_bias"], (P, EXR)))
    put("ones", np.full((P, P), 1.0 / HID, f))

    up_all = np.zeros((2, FC * P, HID), f)
    dn_all = np.zeros((FC * P, HID), f)
    for i, part in enumerate(("gate", "up")):
        up_all[i, :FS] = g[M + "sw_" + part]
        up_all[i, SHARED * P:] = g[M + "w_" + part].reshape(-1, HID)
    dn_all[:FS] = g[M + "sw_down"].T
    dn_all[SHARED * P:] = g[M + "w_down"].transpose(0, 2, 1).reshape(-1, HID)
    w_x = g[A + "w_x"]
    xp = np.zeros((ROWSB, DIB), f)
    xp[:RANKB], xp[ROWSB - BC:] = g[B + "x_proj_w"][:RANKB], g[B + "x_proj_w"][RANKB:]
    arrays = {
        "pack": pack,
        "w_in": tiles(g[A + "w_in"], 16, KC).reshape(8, 2, P, KC * P).transpose(0, 2, 1, 3).reshape(8, P, SLOT),
        "w_x": tiles(w_x[:RANK], 1, UC)[0],
        "w_bc": cols(np.ascontiguousarray(w_x[RANK:].T), UC),
        "w_dt": g[A + "w_dt"].T,
        "x_in_w": tiles(g[B + "in_proj_w"], 4, CC).transpose(1, 0, 2).reshape(P, SLOT),
        "x_proj_w": cols(xp.T, 4),
        "x_dt_w": g[B + "dt_proj_w"].T,
        "w_out": tiles(g[A + "w_out"], KC, UC),
        "w_fgu": np.concatenate([tiles(g[A + "w_gate"], FA, KC), tiles(g[A + "w_up"], FA, KC)], axis=2),
        "w_fdn": g[A + "w_down"].T.reshape(FA, P, HID),
        "w_egu": np.concatenate([tiles(up_all[0], FC, KC), tiles(up_all[1], FC, KC)], axis=2),
        "w_edn": dn_all.reshape(FC, P, HID),
        "w_qk": np.concatenate([tiles(g[E + "Wq"], 1, CC)[0], tiles(g[E + "Wk"], 1, CC)[0]], axis=1),
        "ebias": g[F + "expert_bias"],
        "w_qo": np.concatenate([g[D + "w_qkv"][:, :HEADS * DH].T.reshape(FOLDS, P, HID),
                                g[D + "w_out"].reshape(FOLDS, P, HID)], axis=2),
        "pm": g[D + "pm"].reshape(2, 16, 2, 16, DH).transpose(0, 2, 4, 1, 3).reshape(2, P, 16, 16),
        "xT": g["x"].transpose(0, 2, 1).reshape(SEQS, KC, P, TOK).transpose(0, 2, 1, 3),
        "ctxT": g["ctx_1024"].transpose(0, 2, 1).reshape(SEQS, CC, P, TOK).transpose(0, 2, 1, 3),
    }
    nc = _bacc.Bacc("TRN2", target_bir_lowering=False, num_devices=1)
    feeds, args = {}, []
    for name, a in arrays.items():
        a = np.ascontiguousarray(a)
        feeds["in_" + name] = a
        args.append(nc.dram_tensor("in_" + name, a.shape, _mybir.dt.from_np(a.dtype), kind="ExternalInput").ap())
    args.append(nc.dram_tensor("out", (SEQS, TOK, HID), _mybir.dt.float32, kind="ExternalOutput").ap())
    build(nc, *args)
    r = _run(nc, [feeds], core_ids=[0])
    return r.results[0]["out"]
```
